# Optimizing a Trainium2 kernel written in Bass

```python
import numpy as np
import jax
import jax.numpy as jnp

def _softmax(x, axis=-1):
    return jax.nn.softmax(x, axis=axis)
def _gelu(x):
    return jax.nn.gelu(x, approximate=True)
def _silu(x):
    return jax.nn.silu(x)
def _sigmoid(x):
    return jax.nn.sigmoid(x)
def _layernorm(x, axis=-1, eps=1e-5):
    m = jnp.mean(x, axis=axis, keepdims=True)
    v = jnp.var(x, axis=axis, keepdims=True)
    return (x - m) / jnp.sqrt(v + eps)
def _scatter_add(tgt, idx, src, axis=0):
    return tgt.at[idx].add(src)
def _segment_sum(src, seg, n):
    return jax.ops.segment_sum(src, seg, n)

kernel_name = 'mk_adj_resnorm_d1_adj_512_c69fc3'

def setup_inputs(seed: int = 0):
    np.random.seed(seed)
    _w = jnp.asarray
    def _rec_inputs():
        import jax
        import jax.numpy as jnp
        _gk = jax.random.key(seed)
        x = -0.0002928 + 1 * jax.random.normal(jax.random.fold_in(_gk, 1), (8, 2048, 512), jnp.float32)
        _w = (1.0 + jnp.arange(2048, dtype=jnp.float32)) ** -0.5
        _w = _w / _w.mean()
        _pij = jnp.clip(0.00390625 * _w[:, None] * _w[None, :], 0.0, 1.0)
        _a = jax.random.uniform(jax.random.fold_in(_gk, 2), (8, 2048, 2048)) < _pij
        adj = _a.astype(jnp.int32)
        return x, adj
    x, adj = _rec_inputs()
    def _L0_gnn_setup():
        import jax, jax.numpy as jnp
        import numpy as np
        ALPHA = 0.2
        K_NUM = 16
        NEG_INF = -9000000000000000.0
        key = jax.random.key(seed)
        k1, k2, k3, k4 = jax.random.split(key, 4)
        B, N, F_in, F_out = (4, 2048, 512, 512)
        h = jax.random.normal(k1, (B, N, F_in), dtype=jnp.float32)
        adj = jax.random.randint(k2, (B, N, N), 0, 2, dtype=jnp.int32)

        def xavier(k, shape, gain=1.414):
            fan_in, fan_out = (shape[0], shape[1])
            bound = gain * np.sqrt(6.0 / (fan_in + fan_out))
            return jax.random.uniform(k, shape, jnp.float32, -bound, bound)
        W = xavier(k3, (F_in, F_out))
        a = xavier(k4, (2 * F_out, 1))
        return {'h': h, 'adj': adj, 'W': W, 'a': a}
    _L0_gnn_all = _L0_gnn_setup()
    _L0_gnn_in = {k: v for k, v in _L0_gnn_all.items() if k in ('W', 'a', )}
    del _L0_gnn_all

    return {
        "x": x,
        "adj": adj,
        "L0_gnn_W": _L0_gnn_in["W"],
        "L0_gnn_a": _L0_gnn_in["a"],
    }

def reference(x, adj, L0_gnn_W, L0_gnn_a):
    import jax
    import jax.numpy as jnp
    def _L0_gnn_ref(h, adj, W, a):
        import jax, jax.numpy as jnp
        import numpy as np
        ALPHA = 0.2
        K_NUM = 16
        NEG_INF = -9000000000000000.0
        F_out = W.shape[1]
        Wh = jnp.einsum('bnf,fo->bno', h, W)
        a1, a2 = (a[:F_out, 0], a[F_out:, 0])
        e_src = Wh @ a1
        e_dst = Wh @ a2
        e = e_src[:, :, None] + e_dst[:, None, :]
        e = jnp.where(e > 0, e, ALPHA * e)
        e = jnp.where(adj > 0, e, NEG_INF)
        attention = jax.nn.softmax(e, axis=2)
        topk_vals = jax.lax.top_k(attention, K_NUM)[0]
        kth = topk_vals[:, :, -1:]
        attention = jnp.where(attention < kth, 0.0, attention)
        h_prime = jnp.einsum('bij,bjo->bio', attention, Wh)
        return jax.nn.elu(h_prime)

    x = _layernorm(x + _L0_gnn_ref(x, adj, L0_gnn_W, L0_gnn_a), axis=-1)
    return x


_drawn_inputs = setup_inputs


def setup_inputs(seed=0):
    import zlib

    import numpy as np

    out = dict(_drawn_inputs(seed))
    spreads = {}
    factors = {}
    for name, (base, spread) in spreads.items():
        noise = np.random.default_rng([zlib.crc32(name.encode()), seed]).standard_normal(out[name].shape)
        drawn = base * np.exp(spread * noise) if base else spread * noise
        out[name] = jnp.asarray(drawn.astype(out[name].dtype))
    for name, factor in factors.items():
        out[name] = (out[name] * factor).astype(out[name].dtype)
    return out
```

```python
from contextlib import ExitStack

import concourse.bass as bass
from concourse import mybir

P = 128
FP32 = mybir.dt.float32
FP16 = mybir.dt.float16
I32 = mybir.dt.int32
ALU = mybir.AluOpType
ACT = mybir.ActivationFunctionType
AX = mybir.AxisListType

LRELU_SLOPE = 0.2
LN_EPS = 1e-5
D_SCALE = 2.0 ** -60
NO_NEIGHBOUR = -0.25
FAR = -1.0e30
TOP_EXP = 14
E_SCALE = 2.0 ** TOP_EXP
Y_SCALE = 2.0 ** -25
EXP_MASK = 0x7F800000
EXP_ONE = 1 << 23

LAG_SELECT = 1
LAG_SPLIT = 2
LAG_Y = 7
LAG_ELU = 11
LAG_STATS = 12
LAG_NORM = 13
LAG_STORE = 14


def gat_kernel(nc, x, adj, w, a, out, d_scratch, wa_scratch):
    B, N, F = x.shape
    T = N // P
    CT = 4
    FT = F // P
    HT = T // 2
    NTILE = B * T
    CW = CT * P
    assert FT == CT and N % CW == 0

    x_rows = x.rearrange("b n f -> (b n) f")
    adj_rows = adj.rearrange("b i j -> (b i) j")
    out_rows = out.rearrange("b n f -> (b n) f")
    x_feat = x.rearrange("b (t p) (k f) -> b k p t f", p=P, k=FT)
    w_tiles = w.rearrange("(t p) n -> p t n", p=P)
    a_rows = a.rearrange("(k n) u -> u k n", k=2)

    ctx = ExitStack()
    with ctx:
        def sb(name, shape, dt):
            return ctx.enter_context(nc.sbuf_tensor(name, shape, dt))

        def pb(name, shape, dt):
            return ctx.enter_context(nc.psum_tensor(name, shape, dt))

        def sem(name):
            return ctx.enter_context(nc.semaphore(name))

        adj_t = sb("adj_t", [P, 2, N], I32)
        v_t = sb("v_t", [P, 2, N], FP32)
        e_t = sb("e_t", [P, 2, N], FP32)
        et_f = sb("et_f", [P, 2, HT, P], FP32)
        et_hi = sb("et_hi", [P, 2, T, CW], FP16)
        et_lo = sb("et_lo", [P, 2, T, CW], FP16)
        x_hi = sb("x_hi", [P, T, F], FP16)
        x_lo = sb("x_lo", [P, T, F], FP16)
        x_stage = sb("x_stage", [P, HT, P], FP32)
        x_dot = sb("x_dot", [P, 2, F], FP32)
        res_t = sb("res_t", [P, 4, F], FP32)
        ex_t = sb("ex_t", [P, 2, F], FP32)
        rl_t = sb("rl_t", [P, 2, F], FP32)
        w_hi = sb("w_hi", [P, FT, F], FP16)
        w_lo = sb("w_lo", [P, FT, F], FP16)
        wa_row = sb("wa_row", [P, 2, F], FP32)
        d_row = sb("d_row", [P, N], FP32)
        y_f = sb("y_f", [P, 2, CW], FP32)
        y_hi = sb("y_hi", [P, 2, FT, CW], FP16)
        y_lo = sb("y_lo", [P, 2, FT, CW], FP16)
        dot_junk = sb("dot_junk", [P, 2, F], mybir.dt.bfloat16)
        ident = sb("ident", [P, P], FP32)

        wa_col = sb("wa_col", [P, 2, FT], FP32)
        w_max = sb("w_max", [P, 2], FP32)
        w_exp = sb("w_exp", [P, 3], I32)
        neg_s_next = sb("neg_s_next", [P, T], FP32)
        d_next = sb("d_next", [P, T], FP32)
        xmax_next = sb("xmax_next", [P, T], FP32)
        x_max = sb("x_max", [P, 2], FP32)
        x_exp = sb("x_exp", [P, 3], I32)
        neg_s = sb("neg_s", [P, T], FP32)
        pos_s = sb("pos_s", [P, T], FP32)
        unscale = sb("unscale", [P, 1], FP32)
        top = sb("top", [P, 2, 16], FP32)
        row_scale = sb("row_scale", [P, 2, 3], FP32)
        exp_bias = sb("exp_bias", [P, 2, 2], FP32)
        neg_z = sb("neg_z", [P, 2], FP32)
        neg_m = sb("neg_m", [P, 2], FP32)
        thr_base = sb("thr_base", [P, 2], FP32)
        thr = sb("thr", [P, 2], FP32)
        z_sum = sb("z_sum", [P, 2], FP32)
        z_inv = sb("z_inv", [P, 2], FP32)
        h_scale = sb("h_scale", [P, T], FP32)
        stats = sb("stats", [P, 2, 6], FP32)
        mean_var = sb("mean_var", [P, 2, 2], FP32)
        var_eps = sb("var_eps", [P, 2], FP32)
        rstd = sb("rstd", [P, 2], FP32)
        minus_half = sb("minus_half", [P, 1], FP32)

        tr_ps = pb("tr_ps", [P, T, P], FP32)
        y_ps = [pb(f"y_ps{i}", [P, CW], FP32) for i in range(2)]
        h_ps = [pb(f"h_ps{i}", [P, F], FP32) for i in range(2)]

        adj_in = [sem(f"adj_in{i}") for i in range(2)]
        x_dot_in = [sem(f"x_dot_in{i}") for i in range(2)]
        x_stage_in = sem("x_stage_in")
        res_in = [sem(f"res_in{i}") for i in range(4)]
        stored = [sem(f"stored{i}") for i in range(4)]
        w_in, a_in = sem("w_in"), sem("a_in")
        wa_out, wa_in = sem("wa_out"), sem("wa_in")
        d_out, d_row_in = sem("d_out"), sem("d_row_in")
        w_dot_done = sem("w_dot_done")
        w_max_done, w_exp_done, w_lo_done = sem("w_max_done"), sem("w_exp_done"), sem("w_lo_done")
        x_dot_done = sem("x_dot_done")
        x_red_done = sem("x_red_done")
        s_ready = sem("s_ready")
        x_exp_done, x_scale_ready = sem("x_exp_done"), sem("x_scale_ready")
        unscale_ready = sem("unscale_ready")
        v_ready, top8_ready, row_scale_ready = sem("v_ready"), sem("top8_ready"), sem("row_scale_ready")
        neg_z_ready, neg_m_ready = sem("neg_z_ready"), sem("neg_m_ready")
        rest_ready, top16_ready = sem("rest_ready"), sem("top16_ready")
        thr_base_ready, thr_ready = sem("thr_base_ready"), sem("thr_ready")
        bias_ready, e_joined, e_selected = sem("bias_ready"), sem("e_joined"), sem("e_selected")
        z_inv_ready, h_scale_ready = sem("z_inv_ready"), sem("h_scale_ready")
        stats_ready, mean_var_ready = sem("stats_ready"), sem("mean_var_ready")
        w_hi_done = sem("w_hi_done")
        exps_ready = sem("exps_ready")
        et_copied = sem("et_copied")
        y_copied = sem("y_copied")
        elu_parts_ready = sem("elu_parts_ready")
        x_hi_done = sem("x_hi_done")
        consts_set, ident_ready = sem("consts_set"), sem("ident_ready")
        w_max_all, x_max_all = sem("w_max_all"), sem("x_max_all")
        et_lo_done = sem("et_lo_done")
        y_lo_done = sem("y_lo_done")
        x_scaled, x_lo_done = sem("x_scaled"), sem("x_lo_done")
        exp_part_ready, elu_ready, u_ready = sem("exp_part_ready"), sem("elu_ready"), sem("u_ready")
        var_eps_ready, rstd_ready, normed = sem("var_eps_ready"), sem("rstd_ready"), sem("normed")
        transposed = sem("transposed")
        y_done = sem("y_done")
        h_done = sem("h_done")

        block = ctx.enter_context(nc.Block())

        def wait_apart(engine, semaphore, count):
            engine.wait_ge(semaphore, count)
            engine.nop(nofuse=True)

        dot_tiles, at = [], 0
        for t in range(T):
            n = 0 if t >= 13 else (2 if t % 4 == 3 else 1)
            dot_tiles.append(list(range(at, at + n)))
            at += n
        assert at == T
        DOTS_DONE = 13
        X_SPLIT_AT = 3

        def walk(engine, step, drain):
            for t in range(T):
                step(0, t, lambda lag, t=t: t >= lag, True)
            with engine.Fori(1, B - 1) as b:
                for t in range(T):
                    step(b, t, lambda lag: True, True)
            for t in range(T):
                step(B - 1, t, lambda lag: True, False)
            for t in range(drain):
                step(B, t, lambda lag, t=t: t < lag, False)

        @block.sync
        def _(sp):
            def load_adj(g, slot):
                sp.dma_start(adj_t[:, slot, :], adj_rows[bass.ds(g * P, P), :]).then_inc(adj_in[slot], 16)

            def load_x_dot(b, t, n):
                if not isinstance(n, int) or n >= 2:
                    sp.wait_ge(x_dot_done, n - 1)
                sp.dma_start(x_dot[:, t % 2, :], x_rows[bass.ds((b * T + t) * P, P), :]).then_inc(x_dot_in[t % 2], 16)

            sp.dma_start(e_t[:, 0, :].rearrange("p (t n) -> p t n", t=FT), w_tiles).then_inc(w_in, 16)
            sp.dma_start(e_t[:, 1, 0:2 * F].rearrange("p (k n) -> p k n", k=2),
                         a_rows.to_broadcast([P, 2, F])).then_inc(a_in, 16)
            sp.wait_ge(w_dot_done, 2 * FT)
            with nc.allow_non_contiguous_dma(reason="1024 words once"):
                for k in range(2):
                    sp.dma_start(wa_scratch[k, :].rearrange("(t p) -> p t", p=P),
                                 wa_col[:, k, :]).then_inc(wa_out, 16)
            for t in range(2):
                load_x_dot(0, t, t)
                load_adj(t, t)
            sp.wait_ge(wa_out, 32)
            sp.dma_start(wa_row[:, :, :], wa_scratch.rearrange("(u k) n -> u k n", u=1)
                         .to_broadcast([P, 2, F])).then_inc(wa_in, 16)
            for t in range(2, T):
                load_x_dot(0, t, t)

            def exchange_d_out(b):
                sp.wait_ge(x_dot_done, (b + 1) * T)
                with nc.allow_non_contiguous_dma(reason="2048 words a batch"):
                    sp.dma_start(d_scratch[bass.ds(b, 1), :].rearrange("u (t p) -> p (u t)", p=P),
                                 d_next[:, :]).then_inc(d_out, 16)

            def exchange_d_in(b):
                sp.wait_ge(d_out, 16 * (b + 1))
                sp.dma_start(d_row[:, :], d_scratch[bass.ds(b, 1), :].to_broadcast([P, N])).then_inc(d_row_in, 16)

            exchange_d_out(0)
            exchange_d_in(0)

            def step(b, t, has, more):
                g = b * T + t
                if has(0) and has(1) and (more or t < T - 1):
                    sp.wait_ge(e_joined, g)
                    load_adj(g + 1, (t + 1) % 2)
                if has(LAG_ELU):
                    j = g - LAG_ELU
                    slot = (t - LAG_ELU) % 4
                    if has(LAG_ELU + 4):
                        sp.wait_ge(stored[slot], 16 * ((j - (t - LAG_ELU) % 4) // 4))
                    sp.dma_start(res_t[:, slot, :], x_rows[bass.ds(j * P, P), :]).then_inc(res_in[slot], 16)
                if has(LAG_STORE):
                    j = g - LAG_STORE
                    slot = (t - LAG_STORE) % 4
                    sp.wait_ge(normed, j + 1)
                    sp.dma_start(out_rows[bass.ds(j * P, P), :], res_t[:, slot, :]).then_inc(stored[slot], 16)
                if not has(0):
                    return
                if more:
                    for i in dot_tiles[t]:
                        load_x_dot(b + 1, i, (b + 1) * T + i)
                    if t == DOTS_DONE:
                        exchange_d_out(b + 1)
                if more and t == T - 1:
                    sp.wait_ge(v_ready, g + 1)
                    exchange_d_in(b + 1)
                for h, k in ((1, t - X_SPLIT_AT), (0, t - X_SPLIT_AT + 1)):
                    if 0 <= k < FT:
                        n = (b * FT + k) * 2 + h
                        if k or h or not isinstance(b, int) or b:
                            sp.wait_ge(x_lo_done, n)
                        sp.dma_start(x_stage[:, :, :], x_feat[bass.ds(b, 1), k, :, h * HT:(h + 1) * HT, :]
                                     .rearrange("u p t f -> (u p) t f")).then_inc(x_stage_in, 16)

            walk(sp, step, LAG_STORE)
            for slot in range(4):
                sp.wait_ge(stored[slot], 16 * (NTILE // 4))

        @block.vector
        def _(dve):
            def exponent_scale(exp_tile, max_ap, max_ready, max_count, exp_done, count, done):
                dve.wait_ge(max_ready, max_count)
                nc.vector.tensor_scalar(exp_tile[:, 0:1], max_ap.bitcast(I32), EXP_MASK, None,
                                        ALU.bitwise_and).then_inc(exp_done, 1)
                dve.wait_ge(exp_done, count + 1)
                nc.vector.tensor_scalar(exp_tile[:, 0:1], exp_tile[:, 0:1], float((TOP_EXP + 1) * EXP_ONE), None,
                                        ALU.max).then_inc(exp_done, 1)
                dve.wait_ge(exp_done, count + 2)
                nc.vector.tensor_scalar(exp_tile[:, 2:3], exp_tile[:, 0:1], float(-TOP_EXP * EXP_ONE), None,
                                        ALU.add).then_inc(exp_done, 1)
                nc.vector.tensor_scalar(exp_tile[:, 1:2], exp_tile[:, 0:1], -1.0,
                                        float((254 + TOP_EXP) * EXP_ONE), ALU.mult, ALU.add).then_inc(done, 1)

            w_f = e_t[:, 0, :].rearrange("p (t n) -> p t n", t=FT)
            a_f = e_t[:, 1, 0:2 * F].rearrange("p (k n) -> p k n", k=2)
            dve.wait_ge(w_in, 16)
            dve.wait_ge(a_in, 16)
            for k, factor in enumerate((-1.0, D_SCALE)):
                for t in range(FT):
                    if k or t:
                        dve.wait_ge(w_dot_done, k * FT + t)
                    nc.vector.scalar_tensor_tensor(out=dot_junk[:, 0, :], in0=w_f[:, t, :], scalar=factor,
                                                   in1=a_f[:, k, :], op0=ALU.mult, op1=ALU.mult,
                                                   accum_out=wa_col[:, k, t:t + 1]).then_inc(w_dot_done, 1)
            nc.vector.tensor_reduce(w_max[:, 0:1], e_t[:, 0, :], axis=AX.X, op=ALU.max,
                                    apply_absolute_value=True).then_inc(w_max_done, 1)

            def dots(b, i):
                slot = i % 2
                dve.wait_ge(x_dot_in[slot], 16 * (b * (T // 2) + i // 2 + 1))
                nc.vector.tensor_reduce(xmax_next[:, i:i + 1], x_dot[:, slot, :], axis=AX.X, op=ALU.max,
                                        apply_absolute_value=True)
                if i or not isinstance(b, int) or b:
                    dve.wait_ge(x_dot_done, b * T + i)
                nc.vector.scalar_tensor_tensor(out=dot_junk[:, 0, :], in0=x_dot[:, slot, :], scalar=1.0,
                                               in1=wa_row[:, 0, :], op0=ALU.mult, op1=ALU.mult,
                                               accum_out=neg_s_next[:, i:i + 1])
                nc.vector.scalar_tensor_tensor(out=dot_junk[:, 1, :], in0=x_dot[:, slot, :], scalar=1.0,
                                               in1=wa_row[:, 1, :], op0=ALU.mult, op1=ALU.mult,
                                               accum_out=d_next[:, i:i + 1]).then_inc(x_dot_done, 1)

            def reduce_x_max(b):
                dve.wait_ge(x_dot_done, (b + 1) * T)
                nc.vector.tensor_reduce(x_max[:, 0:1], xmax_next[:, :], axis=AX.X,
                                        op=ALU.max).then_inc(x_red_done, 1)

            exponent_scale(w_exp, w_max[:, 1:2], w_max_all, 1, w_exp_done, 0, w_exp_done)
            dve.wait_ge(w_hi_done, 1)
            nc.vector.scalar_tensor_tensor(out=w_lo[:, :, :].rearrange("p t n -> p (t n)"), in0=e_t[:, 0, :],
                                           scalar=w_exp[:, 1:2].bitcast(FP32),
                                           in1=w_hi[:, :, :].rearrange("p t n -> p (t n)"),
                                           op0=ALU.mult, op1=ALU.subtract).then_inc(w_lo_done, 1)
            dve.wait_ge(wa_in, 16)
            for i in range(T):
                dots(0, i)
            reduce_x_max(0)

            def step(b, t, has, more):
                g = b * T + t
                slot = t % 2
                last = (t - 1) % 2
                if has(0):
                    if t == 0:
                        dve.wait_ge(x_dot_done, (b + 1) * T)
                        if has(1):
                            dve.wait_ge(exps_ready, g)
                        nc.vector.tensor_copy(neg_s[:, :], neg_s_next[:, :])
                        nc.vector.tensor_scalar(pos_s[:, :], neg_s_next[:, :], -1.0, None,
                                                ALU.mult).then_inc(s_ready, 1)
                    if t == 0:
                        dve.wait_ge(d_row_in, 16 * (b + 1))
                    dve.wait_ge(adj_in[slot], 16 * (b * (T // 2) + t // 2 + 1))
                    if has(2):
                        dve.wait_ge(e_selected, g - 1)
                    nc.vector.scalar_tensor_tensor(out=v_t[:, slot, :], in0=adj_t[:, slot, :], scalar=0.5,
                                                   in1=d_row[:, :], op0=ALU.subtract,
                                                   op1=ALU.min).then_inc(v_ready, 1)
                    wait_apart(dve, v_ready, g + 1)
                    nc.vector.max(top[:, slot, 0:8], v_t[:, slot, :]).then_inc(top8_ready, 1)
                    dve.wait_ge(top8_ready, g + 1)
                    nc.vector.tensor_scalar(row_scale[:, slot, 0:1], top[:, slot, 0:1], NO_NEIGHBOUR, -1.0 / D_SCALE,
                                            ALU.is_ge, ALU.mult)
                    nc.vector.tensor_scalar(row_scale[:, slot, 1:2], top[:, slot, 0:1], NO_NEIGHBOUR, 1.0 / D_SCALE,
                                            ALU.is_ge, ALU.mult)
                    nc.vector.tensor_scalar(row_scale[:, slot, 2:3], top[:, slot, 0:1], NO_NEIGHBOUR,
                                            LRELU_SLOPE / D_SCALE, ALU.is_ge, ALU.mult)
                    nc.vector.tensor_scalar(thr_base[:, slot:slot + 1], top[:, slot, 0:1], NO_NEIGHBOUR, FAR,
                                            ALU.is_lt, ALU.mult).then_inc(row_scale_ready, 1)
                if has(LAG_SELECT):
                    dve.wait_ge(exps_ready, g)
                    nc.vector.scalar_tensor_tensor(out=e_t[:, last, :], in0=e_t[:, last, :], scalar=1.0,
                                                   in1=adj_t[:, last, :].bitcast(FP32), op0=ALU.mult, op1=ALU.max,
                                                   accum_out=z_sum[:, last:last + 1]).then_inc(e_joined, 1)
                if has(0) and more:
                    for i in dot_tiles[t][:1]:
                        dots(b + 1, i)
                if has(0):
                    dve.wait_ge(row_scale_ready, g + 1)
                    if t == 0:
                        dve.wait_ge(s_ready, b + 1)
                    nc.vector.scalar_tensor_tensor(out=neg_z[:, slot:slot + 1], in0=top[:, slot, 0:1],
                                                   scalar=row_scale[:, slot, 0:1], in1=neg_s[:, t:t + 1],
                                                   op0=ALU.mult, op1=ALU.add).then_inc(neg_z_ready, 1)
                if has(LAG_STATS) and (has(0) or t < LAG_STATS):
                    j = g - LAG_STATS
                    js = (t - LAG_STATS)
                    dve.wait_ge(u_ready, j + 1)
                    nc.vector.bn_stats(stats[:, js % 2, :], res_t[:, js % 4, :]).then_inc(stats_ready, 1)
                if has(0):
                    dve.wait_ge(neg_z_ready, g + 1)
                    nc.vector.scalar_tensor_tensor(out=neg_m[:, slot:slot + 1], in0=neg_z[:, slot:slot + 1],
                                                   scalar=LRELU_SLOPE, in1=neg_z[:, slot:slot + 1],
                                                   op0=ALU.mult, op1=ALU.min).then_inc(neg_m_ready, 1)
                if has(LAG_STATS):
                    if has(LAG_STATS + 2):
                        dve.wait_ge(normed, j - 1)
                    wait_apart(dve, stats_ready, j + 1)
                    nc.vector.bn_aggr(mean_var[:, js % 2, :], stats[:, js % 2, :]).then_inc(mean_var_ready, 1)
                if has(0):
                    dve.wait_ge(neg_m_ready, g + 1)
                    nc.vector.tensor_tensor(exp_bias[:, slot, 0:1], pos_s[:, t:t + 1], neg_m[:, slot:slot + 1], ALU.add)
                    nc.vector.scalar_tensor_tensor(out=exp_bias[:, slot, 1:2], in0=pos_s[:, t:t + 1],
                                                   scalar=LRELU_SLOPE, in1=neg_m[:, slot:slot + 1],
                                                   op0=ALU.mult, op1=ALU.add).then_inc(bias_ready, 1)
                if has(0) and more:
                    for i in dot_tiles[t][1:]:
                        dots(b + 1, i)
                if has(0) and t == 1:
                    exponent_scale(x_exp, x_max[:, 1:2], x_max_all, b + 1, x_exp_done, 3 * b, x_scale_ready)
                if has(LAG_SELECT):
                    dve.wait_ge(e_joined, g)
                    dve.wait_ge(thr_ready, g)
                    nc.vector.reciprocal(z_inv[:, last:last + 1], z_sum[:, last:last + 1]).then_inc(z_inv_ready, 1)
                    nc.vector.scalar_tensor_tensor(out=e_t[:, last, :], in0=v_t[:, last, :],
                                                   scalar=thr[:, last:last + 1], in1=e_t[:, last, :],
                                                   op0=ALU.is_ge, op1=ALU.mult).then_inc(e_selected, 1)
                if has(0) and t == 1:
                    dve.wait_ge(x_exp_done, 3 * b + 3)
                    nc.vector.tensor_scalar(unscale[:, :], x_exp[:, 2:3].bitcast(FP32),
                                            w_exp[:, 2:3].bitcast(FP32), 1.0 / (E_SCALE * Y_SCALE),
                                            ALU.mult, ALU.mult).then_inc(unscale_ready, 1)
                    dve.wait_ge(unscale_ready, b + 1)
                if has(LAG_SELECT):
                    dve.wait_ge(z_inv_ready, g)
                    nc.vector.tensor_scalar(h_scale[:, (t - 1) % T:(t - 1) % T + 1], z_inv[:, last:last + 1],
                                            unscale[:, 0:1], None, ALU.mult).then_inc(h_scale_ready, 1)
                if has(0):
                    nc.vector.match_replace(out=adj_t[:, slot, :].bitcast(FP32), in_to_replace=top[:, slot, 0:8],
                                            in_values=v_t[:, slot, :], imm_value=FAR).then_inc(rest_ready, 1)
                    wait_apart(dve, rest_ready, g + 1)
                    nc.vector.max(top[:, slot, 8:16], adj_t[:, slot, :].bitcast(FP32)).then_inc(top16_ready, 1)
                    dve.wait_ge(top16_ready, g + 1)
                    nc.vector.scalar_tensor_tensor(out=thr[:, slot:slot + 1], in0=top[:, slot, 15:16],
                                                   scalar=NO_NEIGHBOUR, in1=thr_base[:, slot:slot + 1],
                                                   op0=ALU.max, op1=ALU.add).then_inc(thr_ready, 1)
                if has(0) and more and t == DOTS_DONE:
                    reduce_x_max(b + 1)

            walk(dve, step, LAG_STATS)

        @block.scalar
        def _(act):
            act.wait_ge(w_in, 16)
            act.wait_ge(w_exp_done, 4)
            nc.scalar.activation(w_hi[:, :, :].rearrange("p t n -> p (t n)"), e_t[:, 0, :], ACT.Copy,
                                 scale=w_exp[:, 1:2].bitcast(FP32)).then_inc(w_hi_done, 1)

            def step(b, t, has, more):
                g = b * T + t
                slot = t % 2
                if has(LAG_SPLIT):
                    f = g - LAG_SPLIT
                    tf = t - LAG_SPLIT
                    chunk, col = (tf // CT) % 2, (tf % CT) * P
                    for h in range(2):
                        act.wait_ge(transposed, 2 * f + h + 1)
                        if has(LAG_SPLIT + 1):
                            act.wait_ge(et_lo_done, 2 * f + h - 1)
                        half = tr_ps[:, h * HT:(h + 1) * HT, :]
                        nc.scalar.activation(et_f[:, h, :, :], half, ACT.Copy, scale=E_SCALE)
                        if h == 0 and has(LAG_SPLIT + 2 * CT) and tf % CT == 0:
                            act.wait_ge(y_done, f - CT)
                        nc.scalar.activation(et_hi[:, chunk, h * HT:(h + 1) * HT, col:col + P], half,
                                             ACT.Copy, scale=E_SCALE).then_inc(et_copied, 1)
                if has(LAG_Y):
                    q = g - LAG_Y
                    tq = t - LAG_Y
                    act.wait_ge(y_done, q + 1)
                    if has(LAG_Y + 2):
                        act.wait_ge(y_lo_done, q - 1)
                    nc.scalar.activation(y_f[:, tq % 2, :], y_ps[tq % 2][:, :], ACT.Copy, scale=Y_SCALE)
                    if has(LAG_Y + 2 * CT) and tq % CT == 0:
                        act.wait_ge(h_done, q - CT)
                    nc.scalar.activation(y_hi[:, (tq // CT) % 2, tq % CT, :], y_ps[tq % 2][:, :], ACT.Copy,
                                         scale=Y_SCALE).then_inc(y_copied, 1)
                if has(LAG_ELU):
                    j = g - LAG_ELU
                    tj = t - LAG_ELU
                    act.wait_ge(h_done, j + 1)
                    act.wait_ge(h_scale_ready, j + 1)
                    if has(LAG_ELU + 2):
                        act.wait_ge(u_ready, j - 1)
                    nc.scalar.activation(ex_t[:, tj % 2, :], h_ps[tj % 2][:, :], ACT.Exp,
                                         scale=h_scale[:, tj % T:tj % T + 1])
                    nc.scalar.activation(rl_t[:, tj % 2, :], h_ps[tj % 2][:, :], ACT.Relu,
                                         scale=h_scale[:, tj % T:tj % T + 1]).then_inc(elu_parts_ready, 1)
                if has(0) and X_SPLIT_AT <= t < X_SPLIT_AT + FT:
                    k = t - X_SPLIT_AT
                    if k == 0:
                        act.wait_ge(x_scale_ready, b + 1)
                    if has(T):
                        act.wait_ge(y_done, (b - 1) * T + T - CT + k + 1)
                    for h in range(2):
                        act.wait_ge(x_stage_in, 16 * ((b * FT + k) * 2 + h + 1))
                        nc.scalar.activation(x_hi[:, h * HT:(h + 1) * HT, k * P:(k + 1) * P], x_stage[:, :, :],
                                             ACT.Copy, scale=x_exp[:, 1:2].bitcast(FP32)).then_inc(x_hi_done, 1)
                if has(0):
                    act.wait_ge(bias_ready, g + 1)
                    if has(2):
                        act.wait_ge(transposed, 2 * (g - 1))
                    else:
                        act.wait_ge(w_lo_done, 1)
                    nc.scalar.activation(e_t[:, slot, :], v_t[:, slot, :], ACT.Exp, bias=exp_bias[:, slot, 0:1],
                                         scale=row_scale[:, slot, 1:2])
                    act.wait_ge(top16_ready, g + 1)
                    nc.scalar.activation(adj_t[:, slot, :].bitcast(FP32), v_t[:, slot, :], ACT.Exp,
                                         bias=exp_bias[:, slot, 1:2],
                                         scale=row_scale[:, slot, 2:3]).then_inc(exps_ready, 1)

            walk(act, step, LAG_ELU)

        @block.gpsimd
        def _(pool):
            nc.gpsimd.memset(minus_half[:], -0.5)
            nc.gpsimd.memset(ident[:], 0.0).then_inc(consts_set, 1)
            pool.wait_ge(consts_set, 1)
            nc.gpsimd.affine_select(out=ident[:], in_=ident[:], compare_op=ALU.not_equal, fill=1.0, base=0,
                                    pattern=[[-1, P]], channel_multiplier=1).then_inc(ident_ready, 1)
            pool.wait_ge(w_max_done, 1)
            nc.gpsimd.partition_all_reduce(w_max[:, 1:2], w_max[:, 0:1], P, bass.bass_isa.ReduceOp.max) \
                .then_inc(w_max_all, 1)

            def all_max(b):
                wait_apart(pool, x_red_done, b + 1)
                if not (isinstance(b, int) and b == 0):
                    wait_apart(pool, x_exp_done, 3 * b)
                nc.gpsimd.partition_all_reduce(x_max[:, 1:2], x_max[:, 0:1], P, bass.bass_isa.ReduceOp.max) \
                    .then_inc(x_max_all, 1)

            all_max(0)

            def step(b, t, has, more):
                g = b * T + t
                if has(LAG_SPLIT):
                    f = g - LAG_SPLIT
                    tf = t - LAG_SPLIT
                    chunk, col = (tf // CT) % 2, (tf % CT) * P
                    for h in range(2):
                        pool.wait_ge(et_copied, 2 * f + h + 1)
                        nc.gpsimd.tensor_tensor(et_lo[:, chunk, h * HT:(h + 1) * HT, col:col + P], et_f[:, h, :, :],
                                                et_hi[:, chunk, h * HT:(h + 1) * HT, col:col + P],
                                                ALU.subtract).then_inc(et_lo_done, 1)
                if has(LAG_Y):
                    q = g - LAG_Y
                    tq = t - LAG_Y
                    pool.wait_ge(y_copied, q + 1)
                    nc.gpsimd.tensor_tensor(y_lo[:, (tq // CT) % 2, tq % CT, :], y_f[:, tq % 2, :],
                                            y_hi[:, (tq // CT) % 2, tq % CT, :], ALU.subtract).then_inc(y_lo_done, 1)
                if has(LAG_NORM):
                    j = g - LAG_NORM
                    tj = t - LAG_NORM
                    wait_apart(pool, mean_var_ready, j + 1)
                    nc.gpsimd.tensor_scalar(var_eps[:, tj % 2:tj % 2 + 1], mean_var[:, tj % 2, 1:2], LN_EPS, None,
                                            ALU.add).then_inc(var_eps_ready, 1)
                if has(LAG_ELU):
                    i = g - LAG_ELU
                    ti = t - LAG_ELU
                    wait_apart(pool, elu_parts_ready, i + 1)
                    nc.gpsimd.tensor_scalar(ex_t[:, ti % 2, :], ex_t[:, ti % 2, :], 1.0, -1.0, ALU.min,
                                            ALU.add).then_inc(exp_part_ready, 1)
                if has(LAG_NORM):
                    pool.wait_ge(var_eps_ready, j + 1)
                    nc.gpsimd.tensor_tensor(rstd[:, tj % 2:tj % 2 + 1], var_eps[:, tj % 2:tj % 2 + 1],
                                            minus_half[:, :], ALU.pow).then_inc(rstd_ready, 1)
                if has(LAG_ELU):
                    pool.wait_ge(exp_part_ready, i + 1)
                    nc.gpsimd.tensor_tensor(ex_t[:, ti % 2, :], ex_t[:, ti % 2, :], rl_t[:, ti % 2, :],
                                            ALU.add).then_inc(elu_ready, 1)
                if has(LAG_NORM):
                    wait_apart(pool, rstd_ready, j + 1)
                    nc.gpsimd.tensor_scalar(res_t[:, tj % 4, :], res_t[:, tj % 4, :], mean_var[:, tj % 2, 0:1],
                                            rstd[:, tj % 2:tj % 2 + 1], ALU.subtract, ALU.mult).then_inc(normed, 1)
                if has(LAG_ELU):
                    pool.wait_ge(elu_ready, i + 1)
                    pool.wait_ge(res_in[ti % 4], 16 * ((i - ti % 4) // 4 + 1))
                    nc.gpsimd.tensor_tensor(res_t[:, ti % 4, :], res_t[:, ti % 4, :], ex_t[:, ti % 2, :],
                                            ALU.add).then_inc(u_ready, 1)
                if has(0) and X_SPLIT_AT <= t < X_SPLIT_AT + FT:
                    k = t - X_SPLIT_AT
                    for h in range(2):
                        n = (b * FT + k) * 2 + h
                        wait_apart(pool, x_hi_done, n + 1)
                        nc.gpsimd.tensor_scalar(x_stage[:, :, :], x_stage[:, :, :], x_exp[:, 1:2].bitcast(FP32), None,
                                                ALU.mult).then_inc(x_scaled, 1)
                        pool.wait_ge(x_scaled, n + 1)
                        nc.gpsimd.tensor_tensor(x_lo[:, h * HT:(h + 1) * HT, k * P:(k + 1) * P], x_stage[:, :, :],
                                                x_hi[:, h * HT:(h + 1) * HT, k * P:(k + 1) * P],
                                                ALU.subtract).then_inc(x_lo_done, 1)
                if has(0) and more and t == DOTS_DONE + 1:
                    all_max(b + 1)

            walk(pool, step, LAG_NORM)

        @block.tensor
        def _(pe):
            def transpose_tile(f, tf, first):
                pe.wait_ge(e_selected, f + 1)
                for h in range(2):
                    if not first:
                        pe.wait_ge(et_copied, 2 * f + h - 1)
                    for c in range(h * HT, (h + 1) * HT):
                        last = nc.tensor.transpose(tr_ps[:, c, :], e_t[:, tf % 2, c * P:(c + 1) * P], ident[:, :])
                    last.then_inc(transposed, 1)

            def y_group(q, tq, b, first_two):
                k, chunk = tq % CT, (tq // CT) % 2
                if k == 0:
                    pe.wait_ge(et_lo_done, 2 * (q + CT))
                pe.wait_ge(x_lo_done, 2 * (b * FT + k + 1))
                if not first_two:
                    pe.wait_ge(y_copied, q - 1)
                for c in range(T):
                    xh, xl = x_hi[:, c, k * P:(k + 1) * P], x_lo[:, c, k * P:(k + 1) * P]
                    eh, el = et_hi[:, chunk, c, :], et_lo[:, chunk, c, :]
                    acc = y_ps[tq % 2][:, :]
                    nc.tensor.matmul(acc, xh, eh, start=(c == 0), stop=False)
                    nc.tensor.matmul(acc, xh, el, start=False, stop=False)
                    last = nc.tensor.matmul(acc, xl, eh, start=False, stop=(c == T - 1))
                last.then_inc(y_done, 1)

            def h_tile(j, tj, first_two):
                k, chunk = tj % CT, (tj // CT) % 2
                if k == 0:
                    pe.wait_ge(y_lo_done, j + CT)
                if not first_two:
                    pe.wait_ge(elu_parts_ready, j - 1)
                for c in range(FT):
                    yh, yl = y_hi[:, chunk, c, k * P:(k + 1) * P], y_lo[:, chunk, c, k * P:(k + 1) * P]
                    acc = h_ps[tj % 2][:, :]
                    nc.tensor.matmul(acc, yh, w_hi[:, c, :], start=(c == 0), stop=False)
                    nc.tensor.matmul(acc, yh, w_lo[:, c, :], start=False, stop=False)
                    last = nc.tensor.matmul(acc, yl, w_hi[:, c, :], start=False, stop=(c == FT - 1))
                last.then_inc(h_done, 1)

            pe.wait_ge(ident_ready, 1)
            pe.wait_ge(w_lo_done, 1)
            for f in range(CT):
                transpose_tile(f, f, f == 0)

            U = 2 * CT

            def eight(u, lo=0, hi=0):
                for t in range(U):
                    g = u * U + t
                    if not (hi and t >= U - CT):
                        transpose_tile(g + CT, t, False)
                    y_group(g, t, g // T, bool(lo) and t < 2)
                    if not (lo and t < CT):
                        h_tile(g - CT, t - CT, bool(lo) and t - CT < 2)

            eight(0, lo=1)
            with pe.Fori(1, NTILE // U - 1) as u:
                eight(u)
            eight(NTILE // U - 1, hi=1)
            for t in range(CT):
                h_tile(NTILE - CT + t, U - CT + t, False)


def kernel(**inputs):
    import numpy as np
    import concourse.bacc as bacc
    from concourse.bass_utils import run_bass_kernel_spmd

    nc = bacc.Bacc("TRN2", target_bir_lowering=False, num_devices=1, dynamic_dma_scratch_size=1024)
    arrays, args = {}, []
    for name in ("x", "adj", "L0_gnn_W", "L0_gnn_a"):
        arr = np.ascontiguousarray(inputs[name])
        arrays[f"in_{name}"] = arr
        args.append(nc.dram_tensor(f"in_{name}", arr.shape, mybir.dt.from_np(arr.dtype), kind="ExternalInput").ap())
    B, N, F = inputs["x"].shape
    args.append(nc.dram_tensor("out_0", (B, N, F), FP32, kind="ExternalOutput").ap())
    args.append(nc.dram_tensor("d_scratch", (B, N), FP32, kind="Internal").ap())
    args.append(nc.dram_tensor("wa_scratch", (2, F), FP32, kind="Internal").ap())
    gat_kernel(nc, *args)
    r = run_bass_kernel_spmd(nc, [arrays], core_ids=[0])
    return r.results[0]["out_0"]
```

```python
import math
from contextlib import ExitStack

import concourse.bass as bass
from concourse import mybir

P = 128
FP32 = mybir.dt.float32
FP16 = mybir.dt.float16
I32 = mybir.dt.int32
ALU = mybir.AluOpType
ACT = mybir.ActivationFunctionType
AX = mybir.AxisListType

LRELU_SLOPE = 0.2
LN_EPS = 1e-5
TOP_K = 16
D_SCALE = 2.0 ** -60
NO_NEIGHBOUR = -0.25
FAR = -1.0e30
TOP_EXP = 14
E_LOG_SCALE = TOP_EXP * math.log(2.0)
Y_SCALE = 2.0 ** -25
EXP_MASK = 0x7F800000
EXP_ONE = 1 << 23

LAG_SELECT = 1
LAG_SPLIT = 2
LAG_COPY = 3
LAG_Y = 8
LAG_ELU = 12
LAG_STATS = 13
LAG_STORE = 14


def gat_kernel(nc, x, adj, w, a, out, d_scratch, wa_scratch):
    B, N, F = x.shape
    T = N // P
    CT = 4
    FT = F // P
    HT = T // 2
    NTILE = B * T
    CW = CT * P
    assert FT == CT and N % CW == 0

    x_rows = x.rearrange("b n f -> (b n) f")
    adj_rows = adj.rearrange("b i j -> (b i) j")
    out_rows = out.rearrange("b n f -> (b n) f")
    x_feat = x.rearrange("b (t p) (k f) -> b k p t f", p=P, k=FT)
    w_tiles = w.rearrange("(t p) n -> p t n", p=P)
    a_rows = a.rearrange("(k n) u -> u k n", k=2)

    ctx = ExitStack()
    with ctx:
        def sb(name, shape, dt):
            return ctx.enter_context(nc.sbuf_tensor(name, shape, dt))

        def pb(name, shape, dt):
            return ctx.enter_context(nc.psum_tensor(name, shape, dt))

        def sem(name):
            return ctx.enter_context(nc.semaphore(name))

        adj_t = sb("adj_t", [P, N], I32)
        b_t = sb("b_t", [P, N], FP32)
        v_t = sb("v_t", [P, 2, N], FP32)
        e_t = sb("e_t", [P, 2, N], FP32)
        e_hi = sb("e_hi", [P, N], FP16)
        e_lo = sb("e_lo", [P, N], FP16)
        et_hi = sb("et_hi", [P, 2, T, CW], FP16)
        et_lo = sb("et_lo", [P, 2, T, CW], FP16)
        x_hi = sb("x_hi", [P, T, F], FP16)
        x_lo = sb("x_lo", [P, T, F], FP16)
        x_stage = sb("x_stage", [P, 2, HT, P], FP32)
        x_dot = sb("x_dot", [P, 2, F], FP32)
        res_t = sb("res_t", [P, 2, F], FP32)
        ex_t = sb("ex_t", [P, 4, F], FP32)
        rl_t = sb("rl_t", [P, 2, F], FP32)
        w_hi = sb("w_hi", [P, FT, F], FP16)
        w_lo = sb("w_lo", [P, FT, F], FP16)
        wa_row = sb("wa_row", [P, 2, F], FP32)
        d_row = sb("d_row", [P, N], FP32)
        y_f = sb("y_f", [P, 2, CW], FP32)
        y_hi = sb("y_hi", [P, 2, FT, CW], FP16)
        y_lo = sb("y_lo", [P, 2, FT, CW], FP16)
        dot_junk = sb("dot_junk", [P, F], mybir.dt.bfloat16)
        ident = sb("ident", [P, P], FP16)

        wa_col = sb("wa_col", [P, 2, FT], FP32)
        w_max = sb("w_max", [P, 2], FP32)
        w_exp = sb("w_exp", [P, 3], I32)
        neg_s_next = sb("neg_s_next", [P, T], FP32)
        d_next = sb("d_next", [P, T], FP32)
        xmax_next = sb("xmax_next", [P, T], FP32)
        x_max = sb("x_max", [P, 2], FP32)
        x_exp = sb("x_exp", [P, 3], I32)
        neg_s = sb("neg_s", [P, T], FP32)
        s_off = sb("s_off", [P, 2, T], FP32)
        unscale = sb("unscale", [P, 1], FP32)
        top = sb("top", [P, 2, 16], FP32)
        row_scale = sb("row_scale", [P, 2, 3], FP32)
        degree = sb("degree", [P, 2, 2], FP32)
        crowded = sb("crowded", [P, 2], I32)
        exp_bias = sb("exp_bias", [P, 2, 2], FP32)
        neg_z = sb("neg_z", [P, 2], FP32)
        neg_m = sb("neg_m", [P, 2], FP32)
        thr_base = sb("thr_base", [P, 2], FP32)
        thr = sb("thr", [P, 2], FP32)
        z_sum = sb("z_sum", [P, 2], FP32)
        z_inv = sb("z_inv", [P, 2], FP32)
        h_scale = sb("h_scale", [P, T], FP32)
        stats = sb("stats", [P, 2, 6], FP32)
        mean_var = sb("mean_var", [P, 2, 2], FP32)
        var_eps = sb("var_eps", [P, 2], FP32)
        rstd = sb("rstd", [P, 2], FP32)
        minus_half = sb("minus_half", [P, 1], FP32)

        tr_ps = [pb(f"tr_ps{i}", [P, T, P], FP16) for i in range(2)]
        y_ps = [pb(f"y_ps{i}", [P, CW], FP32) for i in range(2)]
        h_ps = [pb(f"h_ps{i}", [P, F], FP32) for i in range(2)]

        adj_in = sem("adj_in")
        x_dot_in = [sem(f"x_dot_in{i}") for i in range(2)]
        x_stage_in = [sem(f"x_stage_in{i}") for i in range(2)]
        res_in = [sem(f"res_in{i}") for i in range(2)]
        stored = [sem(f"stored{i}") for i in range(4)]
        w_in, a_in = sem("w_in"), sem("a_in")
        wa_out, wa_in = sem("wa_out"), sem("wa_in")
        d_out, d_row_in = sem("d_out"), sem("d_row_in")
        w_dot_done = sem("w_dot_done")
        x_lo_done = sem("x_lo_done")
        exp_part_ready, normed = sem("exp_part_ready"), sem("normed")
        w_max_done, w_exp_done, w_lo_done = sem("w_max_done"), sem("w_exp_done"), sem("w_lo_done")
        x_dot_done = sem("x_dot_done")
        x_red_done = sem("x_red_done")
        s_ready = sem("s_ready")
        x_exp_done, x_scale_ready = sem("x_exp_done"), sem("x_scale_ready")
        unscale_ready = sem("unscale_ready")
        v_ready, top8_ready, row_scale_ready = sem("v_ready"), sem("top8_ready"), sem("row_scale_ready")
        neg_z_ready, neg_m_ready = sem("neg_z_ready"), sem("neg_m_ready")
        selection = sem("selection")
        SELECTION = 3
        bias_ready, e_joined = sem("bias_ready"), sem("e_joined")
        z_inv_ready, h_scale_ready = sem("z_inv_ready"), sem("h_scale_ready")
        stats_ready, mean_var_ready = sem("stats_ready"), sem("mean_var_ready")
        w_hi_done = sem("w_hi_done")
        exps_ready, degree_ready = sem("exps_ready"), sem("degree_ready")
        e_hi_done = sem("e_hi_done")
        et_copied = sem("et_copied")
        y_copied = sem("y_copied")
        elu_parts_ready = sem("elu_parts_ready")
        x_hi_done = sem("x_hi_done")
        consts_set, ident_ready = sem("consts_set"), sem("ident_ready")
        w_max_all, x_max_all = sem("w_max_all"), sem("x_max_all")
        e_lo_done, y_lo_done = sem("e_lo_done"), sem("y_lo_done")
        degree_max, crowded_ready = sem("degree_max"), sem("crowded_ready")
        res_added, u_ready = sem("res_added"), sem("u_ready")
        var_eps_ready, rstd_ready = sem("var_eps_ready"), sem("rstd_ready")
        transposed = sem("transposed")
        y_done = sem("y_done")
        h_done = sem("h_done")

        block = ctx.enter_context(nc.Block())

        def wait_apart(engine, semaphore, count):
            engine.wait_ge(semaphore, count)
            engine.nop(nofuse=True)

        ROW = [t // 2 + (t % 2) * HT for t in range(T)]

        def rows_of(b, t):
            return bass.ds((b * T + (t - t % T) + ROW[t % T]) * P, P)

        def stored_count(g, t, lag):
            return 16 * ((g - lag - (t - lag) % 4) // 4 + 1)

        dot_tiles, at = [], 0
        for t in range(T):
            n = 0 if t >= 13 else (2 if t % 4 == 3 else 1)
            dot_tiles.append(list(range(at, at + n)))
            at += n
        assert at == T
        DOTS_DONE = 13
        X_SPLIT_AT = 4

        def walk(engine, step, drain):
            for t in range(T):
                step(0, t, lambda lag, t=t: t >= lag, True)
            with engine.Fori(1, B - 1) as b:
                for t in range(T):
                    step(b, t, lambda lag: True, True)
            for t in range(T):
                step(B - 1, t, lambda lag: True, False)
            for t in range(drain):
                step(B, t, lambda lag, t=t: t < lag, False)

        @block.sync
        def _(sp):
            def load_adj(b, t):
                sp.dma_start(adj_t[:, :], adj_rows[rows_of(b, t), :]).then_inc(adj_in, 16)

            def load_x_dot(b, t, n):
                if not isinstance(n, int) or n >= 2:
                    sp.wait_ge(x_dot_done, n - 1)
                sp.dma_start(x_dot[:, t % 2, :], x_rows[bass.ds((b * T + t) * P, P), :]).then_inc(x_dot_in[t % 2], 16)

            sp.dma_start(e_t[:, 0, :].rearrange("p (t n) -> p t n", t=FT), w_tiles).then_inc(w_in, 16)
            sp.dma_start(e_t[:, 1, 0:2 * F].rearrange("p (k n) -> p k n", k=2),
                         a_rows.to_broadcast([P, 2, F])).then_inc(a_in, 16)
            sp.wait_ge(w_dot_done, 2 * FT)
            with nc.allow_non_contiguous_dma(reason="1024 words once"):
                for k in range(2):
                    sp.dma_start(wa_scratch[k, :].rearrange("(t p) -> p t", p=P),
                                 wa_col[:, k, :]).then_inc(wa_out, 16)
            for t in range(2):
                load_x_dot(0, t, t)
            load_adj(0, 0)
            sp.wait_ge(wa_out, 32)
            sp.dma_start(wa_row[:, :, :], wa_scratch.rearrange("(u k) n -> u k n", u=1)
                         .to_broadcast([P, 2, F])).then_inc(wa_in, 16)
            for t in range(2, T):
                load_x_dot(0, t, t)

            def exchange_d_out(b):
                sp.wait_ge(x_dot_done, (b + 1) * T)
                with nc.allow_non_contiguous_dma(reason="2048 words a batch"):
                    sp.dma_start(d_scratch[bass.ds(b, 1), :].rearrange("u (t p) -> p (u t)", p=P),
                                 d_next[:, :]).then_inc(d_out, 16)

            def exchange_d_in(b):
                sp.wait_ge(d_out, 16 * (b + 1))
                sp.dma_start(d_row[:, :], d_scratch[bass.ds(b, 1), :].to_broadcast([P, N])).then_inc(d_row_in, 16)

            exchange_d_out(0)
            exchange_d_in(0)

            def step(b, t, has, more):
                g = b * T + t
                if more and t == 0:
                    load_x_dot(b + 1, 0, (b + 1) * T)
                if has(0) and (more or t < T - 1):
                    sp.wait_ge(v_ready, g + 1)
                    load_adj(b, t + 1)
                if has(0) and more:
                    for i in dot_tiles[t + 1] if t + 1 < T else []:
                        load_x_dot(b + 1, i, (b + 1) * T + i)
                    if t == DOTS_DONE:
                        exchange_d_out(b + 1)
                if has(LAG_ELU - 1):
                    j = g - (LAG_ELU - 1)
                    cj = t - (LAG_ELU - 1)
                    if has(LAG_ELU + 1):
                        sp.wait_ge(res_added, j - 1)
                    sp.dma_start(res_t[:, cj % 2, :], x_rows[rows_of(b, cj), :]).then_inc(res_in[cj % 2], 16)
                if has(0):
                    k = t + 1 - X_SPLIT_AT
                    if 0 <= k < FT:
                        for h in range(2):
                            if k or not isinstance(b, int) or b:
                                sp.wait_ge(x_lo_done, (b * FT + k) * 2 - 1 + h)
                            sp.dma_start(x_stage[:, h, :, :], x_feat[bass.ds(b, 1), k, :, h * HT:(h + 1) * HT, :]
                                         .rearrange("u p t f -> (u p) t f")).then_inc(x_stage_in[h], 16)
                if has(0) and more and t == T - 1:
                    sp.wait_ge(v_ready, g + 1)
                    exchange_d_in(b + 1)
                if has(LAG_STORE):
                    j = g - LAG_STORE
                    slot = (t - LAG_STORE) % 4
                    sp.wait_ge(normed, j + 1)
                    sp.dma_start(out_rows[rows_of(b, t - LAG_STORE), :], ex_t[:, slot, :]).then_inc(stored[slot], 16)

            walk(sp, step, LAG_STORE)
            for slot in range(4):
                sp.wait_ge(stored[slot], 16 * (NTILE // 4))

        @block.vector
        def _(dve):
            def exponent_scale(exp_tile, max_ap, max_ready, max_count, exp_done, count, done):
                dve.wait_ge(max_ready, max_count)
                nc.vector.tensor_scalar(exp_tile[:, 0:1], max_ap.bitcast(I32), EXP_MASK, None,
                                        ALU.bitwise_and).then_inc(exp_done, 1)
                dve.wait_ge(exp_done, count + 1)
                nc.vector.tensor_scalar(exp_tile[:, 0:1], exp_tile[:, 0:1], float((TOP_EXP + 1) * EXP_ONE), None,
                                        ALU.max).then_inc(exp_done, 1)
                dve.wait_ge(exp_done, count + 2)
                nc.vector.tensor_scalar(exp_tile[:, 2:3], exp_tile[:, 0:1], float(-TOP_EXP * EXP_ONE), None,
                                        ALU.add).then_inc(exp_done, 1)
                nc.vector.tensor_scalar(exp_tile[:, 1:2], exp_tile[:, 0:1], -1.0,
                                        float((254 + TOP_EXP) * EXP_ONE), ALU.mult, ALU.add).then_inc(done, 1)

            w_f = e_t[:, 0, :].rearrange("p (t n) -> p t n", t=FT)
            a_f = e_t[:, 1, 0:2 * F].rearrange("p (k n) -> p k n", k=2)
            dve.wait_ge(w_in, 16)
            dve.wait_ge(a_in, 16)
            for k, factor in enumerate((-1.0, D_SCALE)):
                for t in range(FT):
                    if k or t:
                        dve.wait_ge(w_dot_done, k * FT + t)
                    nc.vector.scalar_tensor_tensor(out=dot_junk[:, :], in0=w_f[:, t, :], scalar=factor,
                                                   in1=a_f[:, k, :], op0=ALU.mult, op1=ALU.mult,
                                                   accum_out=wa_col[:, k, t:t + 1]).then_inc(w_dot_done, 1)
            nc.vector.tensor_reduce(w_max[:, 0:1], e_t[:, 0, :], axis=AX.X, op=ALU.max,
                                    apply_absolute_value=True).then_inc(w_max_done, 1)

            def dots(b, i):
                slot = i % 2
                dve.wait_ge(x_dot_in[slot], 16 * (b * (T // 2) + i // 2 + 1))
                nc.vector.tensor_reduce(xmax_next[:, i:i + 1], x_dot[:, slot, :], axis=AX.X, op=ALU.max,
                                        apply_absolute_value=True)
                if i or not isinstance(b, int) or b:
                    dve.wait_ge(x_dot_done, b * T + i)
                nc.vector.scalar_tensor_tensor(out=dot_junk[:, :], in0=x_dot[:, slot, :], scalar=1.0,
                                               in1=wa_row[:, 0, :], op0=ALU.mult, op1=ALU.mult,
                                               accum_out=neg_s_next[:, i:i + 1])
                nc.vector.scalar_tensor_tensor(out=x_dot[:, slot, :], in0=x_dot[:, slot, :], scalar=1.0,
                                               in1=wa_row[:, 1, :], op0=ALU.mult, op1=ALU.mult,
                                               accum_out=d_next[:, i:i + 1]).then_inc(x_dot_done, 1)

            def reduce_x_max(b):
                dve.wait_ge(x_dot_done, (b + 1) * T)
                nc.vector.tensor_reduce(x_max[:, 0:1], xmax_next[:, :], axis=AX.X,
                                        op=ALU.max).then_inc(x_red_done, 1)

            exponent_scale(w_exp, w_max[:, 1:2], w_max_all, 1, w_exp_done, 0, w_exp_done)
            dve.wait_ge(w_hi_done, 1)
            nc.vector.scalar_tensor_tensor(out=w_lo[:, :, :].rearrange("p t n -> p (t n)"), in0=e_t[:, 0, :],
                                           scalar=w_exp[:, 1:2].bitcast(FP32),
                                           in1=w_hi[:, :, :].rearrange("p t n -> p (t n)"),
                                           op0=ALU.mult, op1=ALU.subtract).then_inc(w_lo_done, 1)
            dve.wait_ge(wa_in, 16)
            for i in range(T):
                dots(0, i)
            reduce_x_max(0)

            def step(b, t, has, more):
                g = b * T + t
                slot = t % 2
                last = (t - 1) % 2
                if has(0):
                    if t == 0:
                        dve.wait_ge(x_dot_done, (b + 1) * T)
                        if has(1):
                            dve.wait_ge(exps_ready, g)
                        nc.vector.tensor_copy(neg_s[:, :], neg_s_next[:, :])
                        nc.vector.tensor_scalar(s_off[:, 0, :], neg_s_next[:, :], -1.0, E_LOG_SCALE,
                                                ALU.mult, ALU.add)
                        nc.vector.tensor_scalar(s_off[:, 1, :], neg_s_next[:, :], -LRELU_SLOPE, E_LOG_SCALE,
                                                ALU.mult, ALU.add).then_inc(s_ready, 1)
                    if t == 0:
                        dve.wait_ge(d_row_in, 16 * (b + 1))
                    if has(2):
                        dve.wait_ge(h_scale_ready, g - 1)
                    dve.wait_ge(degree_ready, g + 1)
                    nc.vector.scalar_tensor_tensor(out=v_t[:, slot, :], in0=adj_t[:, :], scalar=0.5,
                                                   in1=d_row[:, :], op0=ALU.subtract,
                                                   op1=ALU.min).then_inc(v_ready, 1)
                    wait_apart(dve, v_ready, g + 1)
                    nc.vector.max(top[:, slot, 0:8], v_t[:, slot, :]).then_inc(top8_ready, 1)
                    dve.wait_ge(top8_ready, g + 1)
                    nc.vector.tensor_scalar(row_scale[:, slot, 0:1], top[:, slot, 0:1], NO_NEIGHBOUR, -1.0 / D_SCALE,
                                            ALU.is_ge, ALU.mult)
                    nc.vector.tensor_scalar(row_scale[:, slot, 1:2], top[:, slot, 0:1], NO_NEIGHBOUR, 1.0 / D_SCALE,
                                            ALU.is_ge, ALU.mult)
                    nc.vector.tensor_scalar(row_scale[:, slot, 2:3], top[:, slot, 0:1], NO_NEIGHBOUR,
                                            LRELU_SLOPE / D_SCALE, ALU.is_ge,
                                            ALU.mult).then_inc(row_scale_ready, 1)
                if has(LAG_STORE):
                    i = g - LAG_STORE
                    ni = t - LAG_STORE
                    dve.wait_ge(rstd_ready, i + 1)
                    nc.vector.tensor_scalar(ex_t[:, ni % 4, :], ex_t[:, ni % 4, :], mean_var[:, ni % 2, 0:1],
                                            rstd[:, ni % 2:ni % 2 + 1], ALU.subtract, ALU.mult).then_inc(normed, 1)
                if has(LAG_SELECT):
                    dve.wait_ge(exps_ready, g)
                    nc.vector.scalar_tensor_tensor(out=e_t[:, last, :], in0=e_t[:, last, :], scalar=1.0,
                                                   in1=b_t[:, :], op0=ALU.mult, op1=ALU.max,
                                                   accum_out=z_sum[:, last:last + 1]).then_inc(e_joined, 1)
                if has(0):
                    dve.wait_ge(row_scale_ready, g + 1)
                    if t == 0:
                        dve.wait_ge(s_ready, b + 1)
                    nc.vector.scalar_tensor_tensor(out=neg_z[:, slot:slot + 1], in0=top[:, slot, 0:1],
                                                   scalar=row_scale[:, slot, 0:1], in1=neg_s[:, ROW[t]:ROW[t] + 1],
                                                   op0=ALU.mult, op1=ALU.add).then_inc(neg_z_ready, 1)
                if has(LAG_STATS) and (has(0) or t < LAG_STATS):
                    j = g - LAG_STATS
                    js = (t - LAG_STATS)
                    dve.wait_ge(u_ready, j + 1)
                    nc.vector.bn_stats(stats[:, js % 2, :], ex_t[:, js % 4, :]).then_inc(stats_ready, 1)
                if has(0):
                    dve.wait_ge(neg_z_ready, g + 1)
                    nc.vector.scalar_tensor_tensor(out=neg_m[:, slot:slot + 1], in0=neg_z[:, slot:slot + 1],
                                                   scalar=LRELU_SLOPE, in1=neg_z[:, slot:slot + 1],
                                                   op0=ALU.mult, op1=ALU.min).then_inc(neg_m_ready, 1)
                if has(LAG_STATS):
                    wait_apart(dve, stats_ready, j + 1)
                    nc.vector.bn_aggr(mean_var[:, js % 2, :], stats[:, js % 2, :]).then_inc(mean_var_ready, 1)
                if has(0):
                    dve.wait_ge(neg_m_ready, g + 1)
                    nc.vector.tensor_tensor(exp_bias[:, slot, 0:1], s_off[:, 0, ROW[t]:ROW[t] + 1], neg_m[:, slot:slot + 1], ALU.add)
                    nc.vector.tensor_tensor(exp_bias[:, slot, 1:2], s_off[:, 1, ROW[t]:ROW[t] + 1], neg_m[:, slot:slot + 1],
                                            ALU.add).then_inc(bias_ready, 1)
                if has(0) and t == 1:
                    exponent_scale(x_exp, x_max[:, 1:2], x_max_all, b + 1, x_exp_done, 3 * b, x_scale_ready)
                if has(LAG_SELECT):
                    dve.wait_ge(e_joined, g)
                    nc.vector.reciprocal(z_inv[:, last:last + 1], z_sum[:, last:last + 1]).then_inc(z_inv_ready, 1)
                    wait_apart(dve, crowded_ready, g)
                    with dve.If(dve.value_load(crowded[0:1, last:last + 1], min_val=0, max_val=1)):
                        rest = b_t[:, :]
                        nc.vector.match_replace(out=rest, in_to_replace=top[:, last, 0:8],
                                                in_values=v_t[:, last, :], imm_value=FAR)
                        nc.vector.tensor_scalar(thr_base[:, last:last + 1], top[:, last, 0:1], NO_NEIGHBOUR, FAR,
                                                ALU.is_lt, ALU.mult).then_inc(selection, 1)
                        wait_apart(dve, selection, SELECTION * (g - 1) + 1)
                        nc.vector.max(top[:, last, 8:16], rest).then_inc(selection, 1)
                        dve.wait_ge(selection, SELECTION * (g - 1) + 2)
                        nc.vector.scalar_tensor_tensor(out=thr[:, last:last + 1], in0=top[:, last, 15:16],
                                                       scalar=NO_NEIGHBOUR, in1=thr_base[:, last:last + 1],
                                                       op0=ALU.max, op1=ALU.add).then_inc(selection, 1)
                        dve.wait_ge(selection, SELECTION * g)
                        nc.vector.scalar_tensor_tensor(out=e_t[:, last, :], in0=v_t[:, last, :],
                                                       scalar=thr[:, last:last + 1], in1=e_t[:, last, :],
                                                       op0=ALU.is_ge, op1=ALU.mult)
                    with dve.Else():
                        dve.sem_inc(selection, SELECTION)
                if has(0) and t == 1:
                    dve.wait_ge(x_exp_done, 3 * b + 3)
                    nc.vector.tensor_scalar(unscale[:, :], x_exp[:, 2:3].bitcast(FP32),
                                            w_exp[:, 2:3].bitcast(FP32), 1.0 / Y_SCALE,
                                            ALU.mult, ALU.mult).then_inc(unscale_ready, 1)
                    dve.wait_ge(unscale_ready, b + 1)
                if has(LAG_SELECT):
                    dve.wait_ge(z_inv_ready, g)
                    nc.vector.tensor_scalar(h_scale[:, (t - 1) % T:(t - 1) % T + 1], z_inv[:, last:last + 1],
                                            unscale[:, 0:1], None, ALU.mult).then_inc(h_scale_ready, 1)
                if has(0) and more:
                    for i in dot_tiles[t]:
                        dots(b + 1, i)
                if has(0) and more and t == DOTS_DONE:
                    reduce_x_max(b + 1)
                if has(0) and 0 <= t - X_SPLIT_AT < FT:
                    k = t - X_SPLIT_AT
                    for h in range(2):
                        dve.wait_ge(x_hi_done, (b * FT + k) * 2 + h + 1)
                        nc.vector.scalar_tensor_tensor(out=x_lo[:, h * HT:(h + 1) * HT, k * P:(k + 1) * P],
                                                       in0=x_stage[:, h, :, :], scalar=x_exp[:, 1:2].bitcast(FP32),
                                                       in1=x_hi[:, h * HT:(h + 1) * HT, k * P:(k + 1) * P],
                                                       op0=ALU.mult, op1=ALU.subtract).then_inc(x_lo_done, 1)
                if has(LAG_ELU):
                    i = g - LAG_ELU
                    ni = (t - LAG_ELU) % 4
                    dve.wait_ge(elu_parts_ready, i + 1)
                    nc.vector.tensor_scalar(ex_t[:, ni, :], ex_t[:, ni, :], 1.0, -1.0, ALU.min,
                                            ALU.add).then_inc(exp_part_ready, 1)

            walk(dve, step, LAG_STORE)

        @block.scalar
        def _(act):
            act.wait_ge(w_in, 16)
            act.wait_ge(w_exp_done, 4)
            nc.scalar.activation(w_hi[:, :, :].rearrange("p t n -> p (t n)"), e_t[:, 0, :], ACT.Copy,
                                 scale=w_exp[:, 1:2].bitcast(FP32)).then_inc(w_hi_done, 1)

            def take_degrees(b, t):
                slot = t % 2
                act.wait_ge(adj_in, 16 * (b * T + t + 1))
                if t >= 2 or not isinstance(b, int) or b:
                    act.wait_ge(degree_max, b * T + t - 1)
                nc.scalar.activation(adj_t[:, :], adj_t[:, :], ACT.Relu,
                                     accum_out=degree[:, slot, 0:1]).then_inc(degree_ready, 1)

            take_degrees(0, 0)

            def step(b, t, has, more):
                g = b * T + t
                slot = t % 2
                if has(LAG_SPLIT):
                    f = g - LAG_SPLIT
                    act.wait_ge(h_scale_ready, f + 1)
                    if has(LAG_SPLIT + 1):
                        act.wait_ge(transposed, 2 * f - 1)
                        act.wait_ge(e_lo_done, f)
                    nc.scalar.activation(e_hi[:, :], e_t[:, slot, :], ACT.Copy).then_inc(e_hi_done, 1)
                if has(LAG_COPY):
                    c = g - LAG_COPY
                    tc = t - LAG_COPY
                    chunk, col = (tc // CT) % 2, (tc % CT) * P
                    for h, part in enumerate((et_hi, et_lo)):
                        act.wait_ge(transposed, 2 * c + h + 1)
                        if h == 0 and has(LAG_COPY + 2 * CT) and tc % CT == 0:
                            act.wait_ge(y_done, c - CT)
                        nc.scalar.activation(part[:, chunk, :, col:col + P], tr_ps[h][:, :, :],
                                             ACT.Copy).then_inc(et_copied, 1)
                if has(LAG_Y):
                    q = g - LAG_Y
                    tq = t - LAG_Y
                    act.wait_ge(y_done, q + 1)
                    if has(LAG_Y + 2):
                        act.wait_ge(y_lo_done, q - 1)
                    nc.scalar.activation(y_f[:, tq % 2, :], y_ps[tq % 2][:, :], ACT.Copy, scale=Y_SCALE)
                    if has(LAG_Y + 2 * CT) and tq % CT == 0:
                        act.wait_ge(h_done, q - CT)
                    nc.scalar.activation(y_hi[:, (tq // CT) % 2, tq % CT, :], y_ps[tq % 2][:, :], ACT.Copy,
                                         scale=Y_SCALE).then_inc(y_copied, 1)
                if has(LAG_ELU):
                    j = g - LAG_ELU
                    tj = t - LAG_ELU
                    act.wait_ge(h_done, j + 1)
                    act.wait_ge(h_scale_ready, j + 1)
                    if has(LAG_ELU + 2):
                        act.wait_ge(u_ready, j - 1)
                    if has(LAG_ELU + 4):
                        act.wait_ge(stored[tj % 4], stored_count(g, t, LAG_ELU + 4))
                    nc.scalar.activation(ex_t[:, tj % 4, :], h_ps[tj % 2][:, :], ACT.Exp,
                                         scale=h_scale[:, tj % T:tj % T + 1])
                    nc.scalar.activation(rl_t[:, tj % 2, :], h_ps[tj % 2][:, :], ACT.Relu,
                                         scale=h_scale[:, tj % T:tj % T + 1]).then_inc(elu_parts_ready, 1)
                if has(0) and (more or t < T - 1):
                    take_degrees(b, t + 1)
                if has(0) and X_SPLIT_AT <= t < X_SPLIT_AT + FT:
                    k = t - X_SPLIT_AT
                    if k == 0:
                        act.wait_ge(x_scale_ready, b + 1)
                    if has(T):
                        act.wait_ge(y_done, (b - 1) * T + T - CT + k + 1)
                    for h in range(2):
                        act.wait_ge(x_stage_in[h], 16 * (b * FT + k + 1))
                        nc.scalar.activation(x_hi[:, h * HT:(h + 1) * HT, k * P:(k + 1) * P], x_stage[:, h, :, :],
                                             ACT.Copy, scale=x_exp[:, 1:2].bitcast(FP32)).then_inc(x_hi_done, 1)
                if has(0):
                    act.wait_ge(bias_ready, g + 1)
                    if has(2):
                        act.wait_ge(e_lo_done, g - 1)
                    else:
                        act.wait_ge(w_lo_done, 1)
                    nc.scalar.activation(e_t[:, slot, :], v_t[:, slot, :], ACT.Exp, bias=exp_bias[:, slot, 0:1],
                                         scale=row_scale[:, slot, 1:2])
                    if has(1):
                        act.wait_ge(h_scale_ready, g)
                    nc.scalar.activation(b_t[:, :], v_t[:, slot, :], ACT.Exp,
                                         bias=exp_bias[:, slot, 1:2],
                                         scale=row_scale[:, slot, 2:3]).then_inc(exps_ready, 1)

            walk(act, step, LAG_ELU)

        @block.gpsimd
        def _(pool):
            nc.gpsimd.memset(minus_half[:], -0.5)
            nc.gpsimd.memset(ident[:], 0.0).then_inc(consts_set, 1)
            pool.wait_ge(consts_set, 1)
            nc.gpsimd.affine_select(out=ident[:], in_=ident[:], compare_op=ALU.not_equal, fill=1.0, base=0,
                                    pattern=[[-1, P]], channel_multiplier=1).then_inc(ident_ready, 1)
            pool.wait_ge(w_max_done, 1)
            nc.gpsimd.partition_all_reduce(w_max[:, 1:2], w_max[:, 0:1], P, bass.bass_isa.ReduceOp.max) \
                .then_inc(w_max_all, 1)

            def all_max(b):
                wait_apart(pool, x_red_done, b + 1)
                if not (isinstance(b, int) and b == 0):
                    wait_apart(pool, x_exp_done, 3 * b)
                nc.gpsimd.partition_all_reduce(x_max[:, 1:2], x_max[:, 0:1], P, bass.bass_isa.ReduceOp.max) \
                    .then_inc(x_max_all, 1)

            all_max(0)

            def step(b, t, has, more):
                g = b * T + t
                if has(LAG_STATS):
                    j = g - LAG_STATS
                    tj = t - LAG_STATS
                    pool.wait_ge(exp_part_ready, j + 1)
                    pool.wait_ge(res_added, j + 1)
                    nc.gpsimd.tensor_tensor(ex_t[:, tj % 4, :], ex_t[:, tj % 4, :], rl_t[:, tj % 2, :],
                                            ALU.add).then_inc(u_ready, 1)
                if has(0):
                    slot = t % 2
                    wait_apart(pool, degree_ready, g + 1)
                    nc.gpsimd.partition_all_reduce(degree[:, slot, 1:2], degree[:, slot, 0:1], P,
                                                   bass.bass_isa.ReduceOp.max).then_inc(degree_max, 1)
                    if has(2):
                        pool.wait_ge(h_scale_ready, g - 1)
                    wait_apart(pool, degree_max, g + 1)
                    nc.gpsimd.tensor_scalar(crowded[:, slot:slot + 1], degree[:, slot, 1:2], TOP_K + 0.5, None,
                                            ALU.is_gt).then_inc(crowded_ready, 1)
                if has(LAG_SPLIT):
                    f = g - LAG_SPLIT
                    if has(LAG_SPLIT + 1):
                        pool.wait_ge(transposed, 2 * f)
                    pool.wait_ge(e_hi_done, f + 1)
                    nc.gpsimd.tensor_tensor(e_lo[:, :], e_t[:, t % 2, :], e_hi[:, :],
                                            ALU.subtract).then_inc(e_lo_done, 1)
                if has(LAG_Y):
                    q = g - LAG_Y
                    tq = t - LAG_Y
                    pool.wait_ge(y_copied, q + 1)
                    nc.gpsimd.tensor_tensor(y_lo[:, (tq // CT) % 2, tq % CT, :], y_f[:, tq % 2, :],
                                            y_hi[:, (tq // CT) % 2, tq % CT, :], ALU.subtract).then_inc(y_lo_done, 1)
                if has(LAG_ELU):
                    i = g - LAG_ELU
                    ti = t - LAG_ELU
                    pool.wait_ge(elu_parts_ready, i + 1)
                    pool.wait_ge(res_in[ti % 2], 16 * ((b * T + t - LAG_ELU - ti % 2) // 2 + 1))
                    nc.gpsimd.tensor_tensor(rl_t[:, ti % 2, :], res_t[:, ti % 2, :], rl_t[:, ti % 2, :],
                                            ALU.add).then_inc(res_added, 1)
                if has(LAG_STATS):
                    wait_apart(pool, mean_var_ready, j + 1)
                    nc.gpsimd.tensor_scalar(var_eps[:, tj % 2:tj % 2 + 1], mean_var[:, tj % 2, 1:2], LN_EPS, None,
                                            ALU.add).then_inc(var_eps_ready, 1)
                    pool.wait_ge(var_eps_ready, j + 1)
                    nc.gpsimd.tensor_tensor(rstd[:, tj % 2:tj % 2 + 1], var_eps[:, tj % 2:tj % 2 + 1],
                                            minus_half[:, :], ALU.pow).then_inc(rstd_ready, 1)
                if has(0) and more and t == DOTS_DONE + 1:
                    all_max(b + 1)

            walk(pool, step, LAG_STATS)

        @block.tensor
        def _(pe):
            def transpose_tile(f, first):
                for h, (part, ready) in enumerate(((e_hi, e_hi_done), (e_lo, e_lo_done))):
                    pe.wait_ge(ready, f + 1)
                    if not first:
                        pe.wait_ge(et_copied, 2 * f + h - 1)
                    for c in range(T):
                        last = nc.tensor.transpose(tr_ps[h][:, c, :], part[:, c * P:(c + 1) * P], ident[:, :])
                    last.then_inc(transposed, 1)

            def y_group(q, tq, b, first_two):
                k, chunk = tq % CT, (tq // CT) % 2
                if k == 0:
                    pe.wait_ge(et_copied, 2 * (q + CT))
                pe.wait_ge(x_lo_done, 2 * (b * FT + k + 1))
                if not first_two:
                    pe.wait_ge(y_copied, q - 1)
                for c in range(T):
                    xh, xl = x_hi[:, c, k * P:(k + 1) * P], x_lo[:, c, k * P:(k + 1) * P]
                    eh, el = et_hi[:, chunk, c, :], et_lo[:, chunk, c, :]
                    acc = y_ps[tq % 2][:, :]
                    nc.tensor.matmul(acc, xh, eh, start=(c == 0), stop=False)
                    nc.tensor.matmul(acc, xh, el, start=False, stop=False)
                    last = nc.tensor.matmul(acc, xl, eh, start=False, stop=(c == T - 1))
                last.then_inc(y_done, 1)

            def h_tile(j, tj, first_two):
                k, chunk = tj % CT, (tj // CT) % 2
                if k == 0:
                    pe.wait_ge(y_lo_done, j + CT)
                if not first_two:
                    pe.wait_ge(elu_parts_ready, j - 1)
                for c in range(FT):
                    yh, yl = y_hi[:, chunk, c, k * P:(k + 1) * P], y_lo[:, chunk, c, k * P:(k + 1) * P]
                    acc = h_ps[tj % 2][:, :]
                    nc.tensor.matmul(acc, yh, w_hi[:, c, :], start=(c == 0), stop=False)
                    nc.tensor.matmul(acc, yh, w_lo[:, c, :], start=False, stop=False)
                    last = nc.tensor.matmul(acc, yl, w_hi[:, c, :], start=False, stop=(c == FT - 1))
                last.then_inc(h_done, 1)

            pe.wait_ge(ident_ready, 1)
            pe.wait_ge(w_lo_done, 1)
            for f in range(CT):
                transpose_tile(f, f == 0)

            U = 2 * CT

            def eight(u, lo=0, hi=0):
                for t in range(U):
                    g = u * U + t
                    if not (hi and t >= U - CT):
                        transpose_tile(g + CT, False)
                    y_group(g, t, g // T, bool(lo) and t < 2)
                    if not (lo and t < CT):
                        h_tile(g - CT, t - CT, bool(lo) and t - CT < 2)

            eight(0, lo=1)
            with pe.Fori(1, NTILE // U - 1) as u:
                eight(u)
            eight(NTILE // U - 1, hi=1)
            for t in range(CT):
                h_tile(NTILE - CT + t, U - CT + t, False)


def kernel(**inputs):
    import numpy as np
    import concourse.bacc as bacc
    from concourse.bass_utils import run_bass_kernel_spmd

    nc = bacc.Bacc("TRN2", target_bir_lowering=False, num_devices=1, dynamic_dma_scratch_size=1024)
    arrays, args = {}, []
    for name in ("x", "adj", "L0_gnn_W", "L0_gnn_a"):
        arr = np.ascontiguousarray(inputs[name])
        arrays[f"in_{name}"] = arr
        args.append(nc.dram_tensor(f"in_{name}", arr.shape, mybir.dt.from_np(arr.dtype), kind="ExternalInput").ap())
    B, N, F = inputs["x"].shape
    args.append(nc.dram_tensor("out_0", (B, N, F), FP32, kind="ExternalOutput").ap())
    args.append(nc.dram_tensor("d_scratch", (B, N), FP32, kind="Internal").ap())
    args.append(nc.dram_tensor("wa_scratch", (2, F), FP32, kind="Internal").ap())
    gat_kernel(nc, *args)
    r = run_bass_kernel_spmd(nc, [arrays], core_ids=[0])
    return r.results[0]["out_0"]
```

```python
import math
from contextlib import ExitStack

import concourse.bass as bass
from concourse import mybir

P = 128
FP32 = mybir.dt.float32
FP16 = mybir.dt.float16
I32 = mybir.dt.int32
ALU = mybir.AluOpType
ACT = mybir.ActivationFunctionType
AX = mybir.AxisListType

LRELU_SLOPE = 0.2
LN_EPS = 1e-5
TOP_K = 16
D_SCALE = 2.0 ** -60
NO_NEIGHBOUR = -0.25
FAR = -1.0e30
FAR_UP = 1.0e30
TOP_EXP = 14
E_LOG_SCALE = TOP_EXP * math.log(2.0)
Y_SCALE = 2.0 ** -25
EXP_MASK = 0x7F800000
EXP_ONE = 1 << 23

LAG_EXP = 1
LAG_SELECT = 1
LAG_SPLIT = 2
LAG_COPY = 3
LAG_Y = 8
LAG_ELU = 12
LAG_STATS = 13
LAG_STORE = 14


def gat_kernel(nc, x, adj, w, a, out, d_scratch, wa_scratch):
    B, N, F = x.shape
    T = N // P
    CT = 4
    FT = F // P
    HT = T // 2
    NTILE = B * T
    CW = CT * P
    assert FT == CT and N % CW == 0

    x_rows = x.rearrange("b n f -> (b n) f")
    adj_rows = adj.rearrange("b i j -> (b i) j")
    out_rows = out.rearrange("b n f -> (b n) f")
    x_feat = x.rearrange("b (t p) (k f) -> b k p t f", p=P, k=FT)
    w_tiles = w.rearrange("(t p) n -> p t n", p=P)
    a_rows = a.rearrange("(k n) u -> u k n", k=2)

    ctx = ExitStack()
    with ctx:
        def sb(name, shape, dt):
            return ctx.enter_context(nc.sbuf_tensor(name, shape, dt))

        def pb(name, shape, dt):
            return ctx.enter_context(nc.psum_tensor(name, shape, dt))

        def sem(name):
            return ctx.enter_context(nc.semaphore(name))

        adj_t = sb("adj_t", [P, N], I32)
        v_t = sb("v_t", [P, 2, N], FP32)
        e_t = sb("e_t", [P, 2, N], FP32)
        rest_t = sb("rest_t", [P, N], FP32)
        e_hi = sb("e_hi", [P, N], FP16)
        e_lo = sb("e_lo", [P, N], FP16)
        et_hi = sb("et_hi", [P, 2, T, CW], FP16)
        et_lo = sb("et_lo", [P, 2, T, CW], FP16)
        x_hi = sb("x_hi", [P, T, F], FP16)
        x_lo = sb("x_lo", [P, T, F], FP16)
        x_stage = sb("x_stage", [P, 2, HT, P], FP32)
        x_dot = sb("x_dot", [P, 2, F], FP32)
        res_t = sb("res_t", [P, 2, F], FP32)
        ex_t = sb("ex_t", [P, 4, F], FP32)
        rl_t = sb("rl_t", [P, 2, F], FP32)
        w_hi = sb("w_hi", [P, FT, F], FP16)
        w_lo = sb("w_lo", [P, FT, F], FP16)
        wa_row = sb("wa_row", [P, 2, F], FP32)
        y_f = sb("y_f", [P, 2, CW], FP32)
        y_hi = sb("y_hi", [P, 2, FT, CW], FP16)
        y_lo = sb("y_lo", [P, 2, FT, CW], FP16)
        d_row = sb("d_row", [P, N], FP32)
        dot_junk = sb("dot_junk", [P, F], mybir.dt.uint8)
        abs_junk = sb("abs_junk", [P, F], mybir.dt.uint8)
        ident = sb("ident", [P, P], FP16)

        wa_col = sb("wa_col", [P, 2, FT], FP32)
        w_max = sb("w_max", [P, 2], FP32)
        w_exp = sb("w_exp", [P, 3], I32)
        neg_s_next = sb("neg_s_next", [P, T], FP32)
        d_next = sb("d_next", [P, T], FP32)
        xsum_next = sb("xsum_next", [P, T], FP32)
        x_max = sb("x_max", [P, 2], FP32)
        x_exp = sb("x_exp", [P, 3], I32)
        neg_s = sb("neg_s", [P, T], FP32)
        s_relu = sb("s_relu", [P, T], FP32)
        s_off = sb("s_off", [P, T], FP32)
        unscale = sb("unscale", [P, 1], FP32)
        top = sb("top", [P, 2, 16], FP32)
        row_scale = sb("row_scale", [P, 2, 2], FP32)
        degree = sb("degree", [P, 2], FP32)
        degree_row = sb("degree_row", [1, 2, P], FP32)
        degree_max = sb("degree_max", [1, 1], FP32)
        crowded = sb("crowded", [1, 1], I32)
        exp_bias = sb("exp_bias", [P, 2], FP32)
        minus_half = sb("minus_half", [P, 1], FP32)
        neg = sb("neg", [P, 2, 2], FP32)
        neg_z = neg[:, 0, :]
        neg_m = neg[:, 1, :]
        thr_base = sb("thr_base", [P, 1], FP32)
        thr = sb("thr", [P, 1], FP32)
        z_sum = sb("z_sum", [P, 2], FP32)
        z_inv = sb("z_inv", [P, 2], FP32)
        h_scale = sb("h_scale", [P, T], FP32)
        stats = sb("stats", [P, 2, 6], FP32)
        mean_var = sb("mean_var", [P, 2, 2], FP32)
        norm = sb("norm", [P, 2, 2], FP32)
        rstd, norm_bias = norm[:, 0, :], norm[:, 1, :]

        tr_ps = [pb(f"tr_ps{i}", [P, T, P], FP16) for i in range(2)]
        y_ps = [pb(f"y_ps{i}", [P, CW], FP32) for i in range(2)]
        h_ps = [pb(f"h_ps{i}", [P, F], FP32) for i in range(2)]

        adj_in = sem("adj_in")
        x_dot_in = [sem(f"x_dot_in{i}") for i in range(2)]
        x_stage_in = [sem(f"x_stage_in{i}") for i in range(2)]
        res_in = [sem(f"res_in{i}") for i in range(2)]
        stored = [sem(f"stored{i}") for i in range(4)]
        degree_row_in = [sem(f"degree_row_in{i}") for i in range(2)]
        w_in, a_in = sem("w_in"), sem("a_in")
        x_first_in = [sem(f"x_first_in{i}") for i in range(FT)]
        wa_out, wa_in = sem("wa_out"), sem("wa_in")
        d_out, d_row_in = sem("d_out"), sem("d_row_in")
        w_dot_done = sem("w_dot_done")
        x_lo_done = sem("x_lo_done")
        w_max_done, w_exp_done, w_lo_done = sem("w_max_done"), sem("w_exp_done"), sem("w_lo_done")
        d_dot_done, s_dot_done = sem("d_dot_done"), sem("s_dot_done")
        x_red_done = sem("x_red_done")
        s_ready = sem("s_ready")
        x_exp_done, x_scale_ready = sem("x_exp_done"), sem("x_scale_ready")
        unscale_ready = sem("unscale_ready")
        v_ready, top8_ready, row_scale_ready = sem("v_ready"), sem("top8_ready"), sem("row_scale_ready")
        neg_z_ready, neg_m_ready = sem("neg_z_ready"), sem("neg_m_ready")
        selection = sem("selection")
        SELECTION = 3
        lo_copied = sem("lo_copied")
        bias_part_ready, bias_ready, u_ready = sem("bias_part_ready"), sem("bias_ready"), sem("u_ready")
        degree_max_ready, crowded_ready = sem("degree_max_ready"), sem("crowded_ready")
        z_inv_ready, h_scale_ready = sem("z_inv_ready"), sem("h_scale_ready")
        stats_ready, mean_var_ready = sem("stats_ready"), sem("mean_var_ready")
        var_eps_ready, norm_bias_ready = sem("var_eps_ready"), sem("norm_bias_ready")
        w_hi_done = sem("w_hi_done")
        relu_ready, exp_ready, degree_ready = sem("relu_ready"), sem("exp_ready"), sem("degree_ready")
        hi_copied = sem("hi_copied")
        x_abs_done = sem("x_abs_done")
        d_row_ready = sem("d_row_ready")
        normed = sem("normed")
        e_hi_done = sem("e_hi_done")
        y_copied = sem("y_copied")
        elu_parts_ready = sem("elu_parts_ready")
        x_hi_done = sem("x_hi_done")
        w_max_all, x_max_all = sem("w_max_all"), sem("x_max_all")
        e_lo_done, y_lo_done = sem("e_lo_done"), sem("y_lo_done")
        consts_set, ident_ready = sem("consts_set"), sem("ident_ready")
        l_ready, rstd_ready = sem("l_ready"), sem("rstd_ready")
        res_added = sem("res_added")
        transposed = sem("transposed")
        y_done = sem("y_done")
        h_done = sem("h_done")

        x_first = [et_hi[:, i // 2, (i % 2) * HT:(i % 2 + 1) * HT, :].rearrange("p t n -> p (t n)").bitcast(FP32)
                   .rearrange("p (t f) -> p t f", t=FT) for i in range(FT)]

        block = ctx.enter_context(nc.Block())

        def wait_apart(engine, semaphore, count):
            engine.wait_ge(semaphore, count)
            engine.nop(nofuse=True)

        SPREAD, FIRST = 3, 6
        ROW = [next(r for r in range(T) if (r * SPREAD + FIRST) % T == t) for t in range(T)]

        def rows_of(b, t):
            return bass.ds((b * T + (t - t % T) + ROW[t % T]) * P, P)

        def stored_count(g, t, lag):
            return 16 * ((g - lag - (t - lag) % 4) // 4 + 1)

        dot_tiles, at = [], 0
        for t in range(T):
            n = 0 if t >= 13 else (2 if t in (2, 4, 10) else 1)
            dot_tiles.append(list(range(at, at + n)))
            at += n
        assert at == T
        DOTS_DONE = 13
        X_SPLIT_AT = 5

        def walk(engine, step, drain):
            for t in range(T):
                step(0, t, lambda lag, t=t: t >= lag, True)
            with engine.Fori(1, B - 1) as b:
                for t in range(T):
                    step(b, t, lambda lag: True, True)
            for t in range(T):
                step(B - 1, t, lambda lag: True, False)
            for t in range(drain):
                step(B, t, lambda lag, t=t: t < lag, False)

        @block.sync
        def _(sp):
            def load_adj(b, t):
                sp.dma_start(adj_t[:, :], adj_rows[rows_of(b, t), :]).then_inc(adj_in, 16)

            def load_x_dot(b, t, n):
                if not isinstance(n, int) or n >= T + 2:
                    sp.wait_ge(s_dot_done, n - 1)
                    sp.wait_ge(x_abs_done, n - 1)
                sp.dma_start(x_dot[:, t % 2, :], x_rows[bass.ds((b * T + t) * P, P), :]).then_inc(x_dot_in[t % 2], 16)

            sp.dma_start(rest_t[:, :].rearrange("p (t n) -> p t n", t=FT), w_tiles).then_inc(w_in, 16)
            sp.dma_start(e_t[:, 1, 0:2 * F].rearrange("p (k n) -> p k n", k=2),
                         a_rows.to_broadcast([P, 2, F])).then_inc(a_in, 16)
            def load_x_first(i):
                sp.dma_start(x_first[i], x_rows[i * FT * P:(i + 1) * FT * P, :]
                             .rearrange("(t p) f -> p t f", p=P)).then_inc(x_first_in[i], 16)

            for i in range(2):
                load_x_first(i)
            sp.wait_ge(w_dot_done, 2 * FT)
            with nc.allow_non_contiguous_dma(reason="1024 words once"):
                for k in range(2):
                    sp.dma_start(wa_scratch[k, :].rearrange("(t p) -> p t", p=P),
                                 wa_col[:, k, :]).then_inc(wa_out, 16)
            sp.wait_ge(wa_out, 32)
            sp.dma_start(wa_row[:, :, :], wa_scratch.rearrange("(u k) n -> u k n", u=1)
                         .to_broadcast([P, 2, F])).then_inc(wa_in, 16)
            for i in range(2, FT):
                load_x_first(i)
            load_adj(0, 0)

            def exchange_d_out(b):
                sp.wait_ge(d_dot_done, (b + 1) * T)
                with nc.allow_non_contiguous_dma(reason="2048 words a batch"):
                    sp.dma_start(d_scratch[bass.ds(b, 1), :].rearrange("u (t p) -> p (u t)", p=P),
                                 d_next[:, :]).then_inc(d_out, 16)

            def exchange_d_in(b):
                sp.wait_ge(d_out, 16 * (b + 1))
                if not isinstance(b, int) or b:
                    sp.wait_ge(x_lo_done, b * FT * 2)
                sp.dma_start(x_stage[:, :, :, :].rearrange("p h t f -> p (h t f)"),
                             d_scratch[bass.ds(b, 1), :].to_broadcast([P, N])).then_inc(d_row_in, 16)

            exchange_d_out(0)
            exchange_d_in(0)

            def step(b, t, has, more):
                g = b * T + t
                if more and t == 0:
                    load_x_dot(b + 1, 0, (b + 1) * T)
                if has(0) and (more or t < T - 1):
                    sp.wait_ge(v_ready, g + 1)
                    load_adj(b, t + 1)
                if has(0):
                    if not more and t == T - 1:
                        sp.wait_ge(v_ready, g + 1)
                    sp.wait_ge(degree_ready, g + 1)
                    with nc.allow_non_contiguous_dma(reason="128 words"):
                        sp.dma_start(degree_row[:, t % 2, :],
                                     degree[:, t % 2:t % 2 + 1]).then_inc(degree_row_in[t % 2], 16)
                if has(0) and more:
                    for i in dot_tiles[t + 1] if t + 1 < T else []:
                        load_x_dot(b + 1, i, (b + 1) * T + i)
                    if t == DOTS_DONE:
                        exchange_d_out(b + 1)
                    if t == DOTS_DONE + 1:
                        exchange_d_in(b + 1)
                if has(LAG_ELU - 1):
                    j = g - (LAG_ELU - 1)
                    cj = t - (LAG_ELU - 1)
                    if has(LAG_ELU + 1):
                        sp.wait_ge(res_added, j - 1)
                    sp.dma_start(res_t[:, cj % 2, :], x_rows[rows_of(b, cj), :]).then_inc(res_in[cj % 2], 16)
                if has(0):
                    k = t + 1 - X_SPLIT_AT
                    if 0 <= k < FT:
                        if k == 0:
                            sp.wait_ge(d_row_ready, b + 1)
                        for h in range(2):
                            if k or not isinstance(b, int) or b:
                                sp.wait_ge(x_lo_done, (b * FT + k) * 2 - 1 + h)
                            sp.dma_start(x_stage[:, h, :, :], x_feat[bass.ds(b, 1), k, :, h * HT:(h + 1) * HT, :]
                                         .rearrange("u p t f -> (u p) t f")).then_inc(x_stage_in[h], 16)
                if has(LAG_STORE):
                    j = g - LAG_STORE
                    slot = (t - LAG_STORE) % 4
                    sp.wait_ge(normed, j + 1)
                    sp.dma_start(out_rows[rows_of(b, t - LAG_STORE), :], ex_t[:, slot, :]).then_inc(stored[slot], 16)

            walk(sp, step, LAG_STORE)
            for slot in range(4):
                sp.wait_ge(stored[slot], 16 * (NTILE // 4))

        @block.vector
        def _(dve):
            def exponent_scale(exp_tile, max_ap, max_ready, max_count, exp_done, count, done):
                dve.wait_ge(max_ready, max_count)
                nc.vector.tensor_scalar(exp_tile[:, 0:1], max_ap.bitcast(I32), EXP_MASK, None,
                                        ALU.bitwise_and).then_inc(exp_done, 1)
                dve.wait_ge(exp_done, count + 1)
                nc.vector.tensor_scalar(exp_tile[:, 0:1], exp_tile[:, 0:1], float((TOP_EXP + 1) * EXP_ONE), None,
                                        ALU.max).then_inc(exp_done, 1)
                dve.wait_ge(exp_done, count + 2)
                nc.vector.tensor_scalar(exp_tile[:, 2:3], exp_tile[:, 0:1], float(-TOP_EXP * EXP_ONE), None,
                                        ALU.add).then_inc(exp_done, 1)
                nc.vector.tensor_scalar(exp_tile[:, 1:2], exp_tile[:, 0:1], -1.0,
                                        float((254 + TOP_EXP) * EXP_ONE), ALU.mult, ALU.add).then_inc(done, 1)

            w_f = rest_t[:, :].rearrange("p (t n) -> p t n", t=FT)
            a_f = e_t[:, 1, 0:2 * F].rearrange("p (k n) -> p k n", k=2)
            dve.wait_ge(w_in, 16)
            dve.wait_ge(a_in, 16)
            for k, factor in enumerate((-1.0, D_SCALE)):
                for t in range(FT):
                    if k or t:
                        dve.wait_ge(w_dot_done, k * FT + t)
                    nc.vector.scalar_tensor_tensor(out=dot_junk[:, :], in0=w_f[:, t, :], scalar=factor,
                                                   in1=a_f[:, k, :], op0=ALU.mult, op1=ALU.mult,
                                                   accum_out=wa_col[:, k, t:t + 1]).then_inc(w_dot_done, 1)
            nc.vector.tensor_reduce(w_max[:, 0:1], rest_t[:, :], axis=AX.X, op=ALU.max,
                                    apply_absolute_value=True).then_inc(w_max_done, 1)

            def dots(b, i):
                slot = i % 2
                dve.wait_ge(x_dot_in[slot], 16 * ((b - 1) * (T // 2) + i // 2 + 1))
                dve.wait_ge(s_dot_done, b * T + i)
                nc.vector.scalar_tensor_tensor(out=dot_junk[:, :], in0=x_dot[:, slot, :], scalar=1.0,
                                               in1=wa_row[:, 1, :], op0=ALU.mult, op1=ALU.mult,
                                               accum_out=d_next[:, i:i + 1]).then_inc(d_dot_done, 1)
                dve.wait_ge(d_dot_done, b * T + i + 1)
                nc.vector.scalar_tensor_tensor(out=dot_junk[:, :], in0=x_dot[:, slot, :], scalar=1.0,
                                               in1=wa_row[:, 0, :], op0=ALU.mult, op1=ALU.mult,
                                               accum_out=neg_s_next[:, i:i + 1]).then_inc(s_dot_done, 1)

            def reduce_x_max(b):
                dve.wait_ge(x_abs_done, (b + 1) * T)
                nc.vector.tensor_reduce(x_max[:, 0:1], xsum_next[:, :], axis=AX.X,
                                        op=ALU.max).then_inc(x_red_done, 1)

            exponent_scale(w_exp, w_max[:, 1:2], w_max_all, 1, w_exp_done, 0, w_exp_done)
            dve.wait_ge(wa_in, 16)
            for i in range(T):
                if i:
                    dve.wait_ge(d_dot_done, i)
                dve.wait_ge(x_first_in[i // FT], 16)
                nc.vector.scalar_tensor_tensor(out=dot_junk[:, :], in0=x_first[i // FT][:, i % FT, :], scalar=1.0,
                                               in1=wa_row[:, 1, :], op0=ALU.mult, op1=ALU.mult,
                                               accum_out=d_next[:, i:i + 1]).then_inc(d_dot_done, 1)
            dve.wait_ge(d_dot_done, T)
            for i in range(T):
                if i:
                    dve.wait_ge(s_dot_done, i)
                nc.vector.scalar_tensor_tensor(out=dot_junk[:, :], in0=x_first[i // FT][:, i % FT, :], scalar=1.0,
                                               in1=wa_row[:, 0, :], op0=ALU.mult, op1=ALU.mult,
                                               accum_out=neg_s_next[:, i:i + 1]).then_inc(s_dot_done, 1)
            reduce_x_max(0)

            def step(b, t, has, more):
                g = b * T + t
                slot = t % 2
                last = (t - 1) % 2
                if has(0):
                    if t == 0:
                        dve.wait_ge(s_dot_done, (b + 1) * T)
                        if has(1):
                            dve.wait_ge(relu_ready, g)
                        nc.vector.tensor_copy(neg_s[:, :], neg_s_next[:, :])
                        nc.vector.tensor_scalar(s_relu[:, :], neg_s_next[:, :], -4.0 * D_SCALE, None, ALU.mult)
                        nc.vector.tensor_scalar(s_off[:, :], neg_s_next[:, :], -LRELU_SLOPE, E_LOG_SCALE,
                                                ALU.mult, ALU.add).then_inc(s_ready, 1)
                    if t == 0:
                        dve.wait_ge(d_row_ready, b + 1)
                    if has(2):
                        dve.wait_ge(h_scale_ready, g - 1)
                    dve.wait_ge(degree_ready, g + 1)
                    nc.vector.scalar_tensor_tensor(out=v_t[:, slot, :], in0=adj_t[:, :], scalar=0.5,
                                                   in1=d_row[:, :], op0=ALU.subtract,
                                                   op1=ALU.min).then_inc(v_ready, 1)
                    wait_apart(dve, v_ready, g + 1)
                    nc.vector.max(top[:, slot, 0:8], v_t[:, slot, :]).then_inc(top8_ready, 1)
                    dve.wait_ge(top8_ready, g + 1)
                    if t == 0:
                        dve.wait_ge(s_ready, b + 1)
                    nc.vector.scalar_tensor_tensor(out=neg_z[:, slot:slot + 1], in0=top[:, slot, 0:1],
                                                   scalar=-1.0 / D_SCALE, in1=neg_s[:, ROW[t]:ROW[t] + 1],
                                                   op0=ALU.mult, op1=ALU.add).then_inc(neg_z_ready, 1)
                    nc.vector.tensor_scalar(row_scale[:, slot, 0:1], top[:, slot, 0:1], NO_NEIGHBOUR,
                                            LRELU_SLOPE / D_SCALE, ALU.is_ge, ALU.mult)
                    nc.vector.tensor_scalar(row_scale[:, slot, 1:2], top[:, slot, 0:1], NO_NEIGHBOUR, FAR_UP,
                                            ALU.is_ge, ALU.mult).then_inc(row_scale_ready, 1)
                if t == 0 and not has(1):
                    dve.wait_ge(w_hi_done, 1)
                    nc.vector.scalar_tensor_tensor(out=w_lo[:, :, :].rearrange("p t n -> p (t n)"), in0=rest_t[:, :],
                                                   scalar=w_exp[:, 1:2].bitcast(FP32),
                                                   in1=w_hi[:, :, :].rearrange("p t n -> p (t n)"),
                                                   op0=ALU.mult, op1=ALU.subtract).then_inc(w_lo_done, 1)
                if has(LAG_STORE):
                    i = g - LAG_STORE
                    ni = t - LAG_STORE
                    dve.wait_ge(rstd_ready, i + 1)
                    if has(LAG_STORE + 2):
                        dve.wait_ge(normed, i - 1)
                    nc.vector.scalar_tensor_tensor(out=norm_bias[:, ni % 2:ni % 2 + 1],
                                                   in0=mean_var[:, ni % 2, 0:1], scalar=-1.0,
                                                   in1=rstd[:, ni % 2:ni % 2 + 1], op0=ALU.mult,
                                                   op1=ALU.mult).then_inc(norm_bias_ready, 1)
                if has(LAG_STATS):
                    j = g - LAG_STATS
                    js = t - LAG_STATS
                    dve.wait_ge(res_added, j + 1)
                    nc.vector.scalar_tensor_tensor(out=ex_t[:, js % 4, :], in0=ex_t[:, js % 4, :], scalar=1.0,
                                                   in1=rl_t[:, js % 2, :], op0=ALU.min,
                                                   op1=ALU.add).then_inc(u_ready, 1)
                if has(0):
                    dve.wait_ge(neg_z_ready, g + 1)
                    nc.vector.scalar_tensor_tensor(out=neg_m[:, slot:slot + 1], in0=neg_z[:, slot:slot + 1],
                                                   scalar=LRELU_SLOPE, in1=neg_z[:, slot:slot + 1],
                                                   op0=ALU.mult, op1=ALU.min).then_inc(neg_m_ready, 1)
                if has(LAG_STATS):
                    dve.wait_ge(u_ready, j + 1)
                    nc.vector.bn_stats(stats[:, js % 2, :], ex_t[:, js % 4, :]).then_inc(stats_ready, 1)
                if has(LAG_STATS):
                    wait_apart(dve, stats_ready, j + 1)
                    nc.vector.bn_aggr(mean_var[:, js % 2, :], stats[:, js % 2, :]).then_inc(mean_var_ready, 1)
                if has(0):
                    dve.wait_ge(neg_m_ready, g + 1)
                    nc.vector.tensor_tensor(exp_bias[:, slot:slot + 1], s_off[:, ROW[t]:ROW[t] + 1],
                                            neg_m[:, slot:slot + 1], ALU.add).then_inc(bias_part_ready, 1)
                    dve.wait_ge(row_scale_ready, g + 1)
                    dve.wait_ge(bias_part_ready, g + 1)
                    nc.vector.scalar_tensor_tensor(out=exp_bias[:, slot:slot + 1], in0=row_scale[:, slot, 1:2],
                                                   scalar=E_LOG_SCALE, in1=exp_bias[:, slot:slot + 1],
                                                   op0=ALU.add, op1=ALU.min).then_inc(bias_ready, 1)
                if has(0) and t == 1:
                    exponent_scale(x_exp, x_max[:, 1:2], x_max_all, b + 1, x_exp_done, 3 * b, x_scale_ready)
                if has(LAG_STATS):
                    dve.wait_ge(mean_var_ready, j + 1)
                    nc.vector.tensor_scalar(mean_var[:, js % 2, 1:2], mean_var[:, js % 2, 1:2], LN_EPS, None,
                                            ALU.add).then_inc(var_eps_ready, 1)
                if has(LAG_COPY):
                    c = g - LAG_COPY
                    tc = t - LAG_COPY
                    chunk, col = (tc // CT) % 2, (tc % CT) * P
                    dve.wait_ge(transposed, 2 * c + 2)
                    if has(LAG_COPY + 2 * CT) and tc % CT == 0:
                        dve.wait_ge(y_done, c - CT)
                    nc.vector.tensor_copy(et_lo[:, chunk, :, col:col + P],
                                          tr_ps[1][:, :, :]).then_inc(lo_copied, 1)
                if has(LAG_SELECT):
                    dve.wait_ge(degree_row_in[last], 16 * ((g - 1 - last) // 2 + 1))
                    nc.vector.tensor_reduce(degree_max[:, 0:1], degree_row[:, last, :], axis=AX.X,
                                            op=ALU.max).then_inc(degree_max_ready, 1)
                    dve.wait_ge(degree_max_ready, g)
                    nc.vector.tensor_scalar(crowded[:, 0:1], degree_max[:, 0:1], TOP_K + 0.5,
                                            None, ALU.is_gt).then_inc(crowded_ready, 1)
                    dve.wait_ge(exp_ready, g)
                    nc.vector.reciprocal(z_inv[:, last:last + 1], z_sum[:, last:last + 1]).then_inc(z_inv_ready, 1)
                    if not has(2):
                        dve.wait_ge(w_lo_done, 1)
                    wait_apart(dve, crowded_ready, g)
                    with dve.If(dve.value_load(crowded[0:1, 0:1], min_val=0, max_val=1)):
                        rest = rest_t[:, :]
                        nc.vector.match_replace(out=rest, in_to_replace=top[:, last, 0:8],
                                                in_values=v_t[:, last, :], imm_value=FAR)
                        nc.vector.tensor_scalar(thr_base[:, 0:1], top[:, last, 0:1], NO_NEIGHBOUR, FAR,
                                                ALU.is_lt, ALU.mult).then_inc(selection, 1)
                        wait_apart(dve, selection, SELECTION * (g - 1) + 1)
                        nc.vector.max(top[:, last, 8:16], rest).then_inc(selection, 1)
                        dve.wait_ge(selection, SELECTION * (g - 1) + 2)
                        nc.vector.scalar_tensor_tensor(out=thr[:, 0:1], in0=top[:, last, 15:16],
                                                       scalar=NO_NEIGHBOUR, in1=thr_base[:, 0:1],
                                                       op0=ALU.max, op1=ALU.add).then_inc(selection, 1)
                        dve.wait_ge(selection, SELECTION * g)
                        nc.vector.scalar_tensor_tensor(out=e_t[:, last, :], in0=v_t[:, last, :],
                                                       scalar=thr[:, 0:1], in1=e_t[:, last, :],
                                                       op0=ALU.is_ge, op1=ALU.mult)
                    with dve.Else():
                        dve.sem_inc(selection, SELECTION)
                if has(0) and t == 1:
                    dve.wait_ge(x_exp_done, 3 * b + 3)
                    nc.vector.tensor_scalar(unscale[:, :], x_exp[:, 2:3].bitcast(FP32),
                                            w_exp[:, 2:3].bitcast(FP32), 1.0 / Y_SCALE,
                                            ALU.mult, ALU.mult).then_inc(unscale_ready, 1)
                    dve.wait_ge(unscale_ready, b + 1)
                if has(LAG_SELECT):
                    dve.wait_ge(z_inv_ready, g)
                    nc.vector.tensor_scalar(h_scale[:, (t - 1) % T:(t - 1) % T + 1], z_inv[:, last:last + 1],
                                            unscale[:, 0:1], None, ALU.mult).then_inc(h_scale_ready, 1)
                if has(0) and more:
                    for i in dot_tiles[t]:
                        dots(b + 1, i)
                if has(0) and more and t == DOTS_DONE:
                    reduce_x_max(b + 1)
                if has(0) and 0 <= t - X_SPLIT_AT < FT:
                    k = t - X_SPLIT_AT
                    for h in range(2):
                        dve.wait_ge(x_hi_done, (b * FT + k) * 2 + h + 1)
                        nc.vector.scalar_tensor_tensor(out=x_lo[:, h * HT:(h + 1) * HT, k * P:(k + 1) * P],
                                                       in0=x_stage[:, h, :, :], scalar=x_exp[:, 1:2].bitcast(FP32),
                                                       in1=x_hi[:, h * HT:(h + 1) * HT, k * P:(k + 1) * P],
                                                       op0=ALU.mult, op1=ALU.subtract).then_inc(x_lo_done, 1)
            walk(dve, step, LAG_STORE)

        @block.scalar
        def _(act):
            act.wait_ge(w_in, 16)
            act.wait_ge(w_exp_done, 4)
            nc.scalar.activation(w_hi[:, :, :].rearrange("p t n -> p (t n)"), rest_t[:, :], ACT.Copy,
                                 scale=w_exp[:, 1:2].bitcast(FP32)).then_inc(w_hi_done, 1)

            def take_degrees(b, t):
                slot = t % 2
                act.wait_ge(adj_in, 16 * (b * T + t + 1))
                if t >= 2 or not isinstance(b, int) or b:
                    act.wait_ge(degree_row_in[slot], 16 * (b * (T // 2) + t // 2))
                nc.scalar.activation(adj_t[:, :], adj_t[:, :], ACT.Relu,
                                     accum_out=degree[:, slot:slot + 1]).then_inc(degree_ready, 1)

            def abs_sums(n, i, x_tile, x_in, count):
                act.wait_ge(x_in, count)
                if not isinstance(n, int) or n:
                    act.wait_ge(x_abs_done, n)
                nc.scalar.activation(abs_junk[:, :], x_tile, ACT.Abs,
                                     accum_out=xsum_next[:, i:i + 1]).then_inc(x_abs_done, 1)

            def copy_d_row(b):
                act.wait_ge(d_row_in, 16 * (b + 1))
                nc.scalar.activation(d_row[:, :], x_stage[:, :, :, :].rearrange("p h t f -> p (h t f)"),
                                     ACT.Copy).then_inc(d_row_ready, 1)

            for i in range(T):
                abs_sums(i, i, x_first[i // FT][:, i % FT, :], x_first_in[i // FT], 16)
            take_degrees(0, 0)
            copy_d_row(0)

            def step(b, t, has, more):
                g = b * T + t
                slot = t % 2
                if has(LAG_SPLIT):
                    f = g - LAG_SPLIT
                    act.wait_ge(h_scale_ready, f + 1)
                    if has(LAG_SPLIT + 1):
                        act.wait_ge(transposed, 2 * f - 1)
                        act.wait_ge(e_lo_done, f)
                    nc.scalar.activation(e_hi[:, :], e_t[:, slot, :], ACT.Copy).then_inc(e_hi_done, 1)
                if has(LAG_COPY):
                    c = g - LAG_COPY
                    tc = t - LAG_COPY
                    chunk, col = (tc // CT) % 2, (tc % CT) * P
                    act.wait_ge(transposed, 2 * c + 1)
                    if has(LAG_COPY + 2 * CT) and tc % CT == 0:
                        act.wait_ge(y_done, c - CT)
                    nc.scalar.activation(et_hi[:, chunk, :, col:col + P], tr_ps[0][:, :, :],
                                         ACT.Copy).then_inc(hi_copied, 1)
                if has(LAG_Y):
                    q = g - LAG_Y
                    tq = t - LAG_Y
                    act.wait_ge(y_done, q + 1)
                    if has(LAG_Y + 2):
                        act.wait_ge(y_lo_done, q - 1)
                    nc.scalar.activation(y_f[:, tq % 2, :], y_ps[tq % 2][:, :], ACT.Copy, scale=Y_SCALE)
                    if has(LAG_Y + 2 * CT) and tq % CT == 0:
                        act.wait_ge(h_done, q - CT)
                    nc.scalar.activation(y_hi[:, (tq // CT) % 2, tq % CT, :], y_ps[tq % 2][:, :], ACT.Copy,
                                         scale=Y_SCALE).then_inc(y_copied, 1)
                if has(LAG_EXP):
                    act.wait_ge(bias_ready, g)
                    act.wait_ge(l_ready, g)
                    nc.scalar.activation(e_t[:, 1 - slot, :], e_t[:, 1 - slot, :], ACT.Exp,
                                         bias=exp_bias[:, 1 - slot:2 - slot], scale=row_scale[:, 1 - slot, 0:1],
                                         accum_out=z_sum[:, 1 - slot:2 - slot]).then_inc(exp_ready, 1)
                if has(0):
                    act.wait_ge(v_ready, g + 1)
                    if t == 0:
                        act.wait_ge(s_ready, b + 1)
                    if has(2):
                        act.wait_ge(e_lo_done, g - 1)
                    else:
                        act.wait_ge(w_dot_done, 2 * FT)
                    nc.scalar.activation(e_t[:, slot, :], v_t[:, slot, :], ACT.Relu,
                                         bias=s_relu[:, ROW[t]:ROW[t] + 1], scale=4.0).then_inc(relu_ready, 1)
                if has(0) and more and t == T - 1:
                    copy_d_row(b + 1)
                if has(LAG_ELU):
                    j = g - LAG_ELU
                    tj = t - LAG_ELU
                    act.wait_ge(h_done, j + 1)
                    act.wait_ge(h_scale_ready, j + 1)
                    if has(LAG_ELU + 2):
                        act.wait_ge(u_ready, j - 1)
                    if has(LAG_ELU + 4):
                        act.wait_ge(stored[tj % 4], stored_count(g, t, LAG_ELU + 4))
                    nc.scalar.activation(ex_t[:, tj % 4, :], h_ps[tj % 2][:, :], ACT.Exp,
                                         scale=h_scale[:, tj % T:tj % T + 1])
                    nc.scalar.activation(rl_t[:, tj % 2, :], h_ps[tj % 2][:, :], ACT.Relu,
                                         scale=h_scale[:, tj % T:tj % T + 1]).then_inc(elu_parts_ready, 1)
                if has(LAG_STORE):
                    i = g - LAG_STORE
                    ni = (t - LAG_STORE) % 4
                    act.wait_ge(norm_bias_ready, i + 1)
                    nc.scalar.activation(ex_t[:, ni, :], ex_t[:, ni, :], ACT.Identity, bias=norm_bias[:, ni % 2:ni % 2 + 1],
                                         scale=rstd[:, ni % 2:ni % 2 + 1]).then_inc(normed, 1)
                if has(0) and (more or t < T - 1):
                    take_degrees(b, t + 1)
                if has(0) and more:
                    for i in dot_tiles[t]:
                        abs_sums((b + 1) * T + i, i, x_dot[:, i % 2, :], x_dot_in[i % 2],
                                 16 * (b * (T // 2) + i // 2 + 1))
                if has(0) and X_SPLIT_AT <= t < X_SPLIT_AT + FT:
                    k = t - X_SPLIT_AT
                    if k == 0:
                        act.wait_ge(x_scale_ready, b + 1)
                    if has(T):
                        act.wait_ge(y_done, (b - 1) * T + T - CT + k + 1)
                    for h in range(2):
                        act.wait_ge(x_stage_in[h], 16 * (b * FT + k + 1))
                        nc.scalar.activation(x_hi[:, h * HT:(h + 1) * HT, k * P:(k + 1) * P], x_stage[:, h, :, :],
                                             ACT.Copy, scale=x_exp[:, 1:2].bitcast(FP32)).then_inc(x_hi_done, 1)

            walk(act, step, LAG_STORE)

        @block.gpsimd
        def _(pool):
            nc.gpsimd.memset(minus_half[:, :], -0.5)
            nc.gpsimd.memset(ident[:], 0.0).then_inc(consts_set, 1)
            pool.wait_ge(consts_set, 1)
            nc.gpsimd.affine_select(out=ident[:], in_=ident[:], compare_op=ALU.not_equal, fill=1.0, base=0,
                                    pattern=[[-1, P]], channel_multiplier=1).then_inc(ident_ready, 1)
            pool.wait_ge(w_max_done, 1)
            nc.gpsimd.partition_all_reduce(w_max[:, 1:2], w_max[:, 0:1], P, bass.bass_isa.ReduceOp.max) \
                .then_inc(w_max_all, 1)

            def all_max(b):
                wait_apart(pool, x_red_done, b + 1)
                if not (isinstance(b, int) and b == 0):
                    wait_apart(pool, x_exp_done, 3 * b)
                nc.gpsimd.partition_all_reduce(x_max[:, 1:2], x_max[:, 0:1], P, bass.bass_isa.ReduceOp.max) \
                    .then_inc(x_max_all, 1)

            all_max(0)

            def step(b, t, has, more):
                g = b * T + t
                if has(LAG_SPLIT):
                    f = g - LAG_SPLIT
                    if has(LAG_SPLIT + 1):
                        pool.wait_ge(transposed, 2 * f)
                    pool.wait_ge(e_hi_done, f + 1)
                    nc.gpsimd.tensor_tensor(e_lo[:, :], e_t[:, t % 2, :], e_hi[:, :],
                                            ALU.subtract).then_inc(e_lo_done, 1)
                if has(LAG_Y):
                    q = g - LAG_Y
                    tq = t - LAG_Y
                    pool.wait_ge(y_copied, q + 1)
                    nc.gpsimd.tensor_tensor(y_lo[:, (tq // CT) % 2, tq % CT, :], y_f[:, tq % 2, :],
                                            y_hi[:, (tq // CT) % 2, tq % CT, :], ALU.subtract).then_inc(y_lo_done, 1)
                if has(0):
                    pool.wait_ge(relu_ready, g + 1)
                    nc.gpsimd.tensor_tensor(e_t[:, t % 2, :], v_t[:, t % 2, :], e_t[:, t % 2, :], ALU.add).then_inc(l_ready, 1)
                if has(LAG_ELU):
                    i = g - LAG_ELU
                    ti = t - LAG_ELU
                    pool.wait_ge(elu_parts_ready, i + 1)
                    pool.wait_ge(res_in[ti % 2], 16 * ((b * T + t - LAG_ELU - ti % 2) // 2 + 1))
                    nc.gpsimd.tensor_tensor(rl_t[:, ti % 2, :], res_t[:, ti % 2, :], rl_t[:, ti % 2, :],
                                            ALU.add).then_inc(res_added, 1)
                if has(LAG_STATS):
                    j = g - LAG_STATS
                    tj = t - LAG_STATS
                    pool.wait_ge(var_eps_ready, j + 1)
                    if has(LAG_STATS + 2):
                        pool.wait_ge(normed, j - 1)
                    nc.gpsimd.tensor_tensor(rstd[:, tj % 2:tj % 2 + 1], mean_var[:, tj % 2, 1:2],
                                            minus_half[:, :], ALU.pow).then_inc(rstd_ready, 1)
                if has(0) and more and t == DOTS_DONE + 1:
                    all_max(b + 1)

            walk(pool, step, LAG_STATS)

        @block.tensor
        def _(pe):
            def transpose_tile(f, first):
                for h, (part, ready, copied) in enumerate(((e_hi, e_hi_done, hi_copied), (e_lo, e_lo_done, lo_copied))):
                    pe.wait_ge(ready, f + 1)
                    if not first:
                        pe.wait_ge(copied, f)
                    for c in range(T):
                        last = nc.tensor.transpose(tr_ps[h][:, c, :], part[:, c * P:(c + 1) * P], ident[:, :])
                    last.then_inc(transposed, 1)

            def y_group(q, tq, b, first_two):
                k, chunk = tq % CT, (tq // CT) % 2
                if k == 0:
                    pe.wait_ge(hi_copied, q + CT)
                    pe.wait_ge(lo_copied, q + CT)
                pe.wait_ge(x_lo_done, 2 * (b * FT + k + 1))
                if not first_two:
                    pe.wait_ge(y_copied, q - 1)
                for c in range(T):
                    xh, xl = x_hi[:, c, k * P:(k + 1) * P], x_lo[:, c, k * P:(k + 1) * P]
                    eh, el = et_hi[:, chunk, c, :], et_lo[:, chunk, c, :]
                    acc = y_ps[tq % 2][:, :]
                    nc.tensor.matmul(acc, xh, eh, start=(c == 0), stop=False)
                    nc.tensor.matmul(acc, xh, el, start=False, stop=False)
                    last = nc.tensor.matmul(acc, xl, eh, start=False, stop=(c == T - 1))
                last.then_inc(y_done, 1)

            def h_tile(j, tj, first_two):
                k, chunk = tj % CT, (tj // CT) % 2
                if first_two:
                    pe.wait_ge(w_lo_done, 1)
                if k == 0:
                    pe.wait_ge(y_lo_done, j + CT)
                if not first_two:
                    pe.wait_ge(elu_parts_ready, j - 1)
                for c in range(FT):
                    yh, yl = y_hi[:, chunk, c, k * P:(k + 1) * P], y_lo[:, chunk, c, k * P:(k + 1) * P]
                    acc = h_ps[tj % 2][:, :]
                    nc.tensor.matmul(acc, yh, w_hi[:, c, :], start=(c == 0), stop=False)
                    nc.tensor.matmul(acc, yh, w_lo[:, c, :], start=False, stop=False)
                    last = nc.tensor.matmul(acc, yl, w_hi[:, c, :], start=False, stop=(c == FT - 1))
                last.then_inc(h_done, 1)

            pe.wait_ge(ident_ready, 1)
            for f in range(CT):
                transpose_tile(f, f == 0)

            U = 2 * CT

            def eight(u, lo=0, hi=0):
                for t in range(U):
                    g = u * U + t
                    if lo and t == 0:
                        y_group(g, t, 0, True)
                    if not (hi and t >= U - CT):
                        transpose_tile(g + CT, False)
                    if not (lo and t == 0):
                        y_group(g, t, g // T, bool(lo) and t < 2)
                    if not (lo and t < CT):
                        h_tile(g - CT, t - CT, bool(lo) and t - CT < 2)

            eight(0, lo=1)
            with pe.Fori(1, NTILE // U - 1) as u:
                eight(u)
            eight(NTILE // U - 1, hi=1)
            for t in range(CT):
                h_tile(NTILE - CT + t, U - CT + t, False)


def kernel(**inputs):
    import numpy as np
    import concourse.bacc as bacc
    from concourse.bass_utils import run_bass_kernel_spmd

    nc = bacc.Bacc("TRN2", target_bir_lowering=False, num_devices=1, dynamic_dma_scratch_size=128)
    arrays, args = {}, []
    for name in ("x", "adj", "L0_gnn_W", "L0_gnn_a"):
        arr = np.ascontiguousarray(inputs[name])
        arrays[f"in_{name}"] = arr
        args.append(nc.dram_tensor(f"in_{name}", arr.shape, mybir.dt.from_np(arr.dtype), kind="ExternalInput").ap())
    B, N, F = inputs["x"].shape
    args.append(nc.dram_tensor("out_0", (B, N, F), FP32, kind="ExternalOutput").ap())
    args.append(nc.dram_tensor("d_scratch", (B, N), FP32, kind="Internal").ap())
    args.append(nc.dram_tensor("wa_scratch", (2, F), FP32, kind="Internal").ap())
    gat_kernel(nc, *args)
    r = run_bass_kernel_spmd(nc, [arrays], core_ids=[0])
    return r.results[0]["out_0"]
```
